# Optimizing a Trainium2 kernel written in Bass

```python
import numpy as np
import jax
import jax.numpy as jnp

def _softmax(x, axis=-1):
    return jax.nn.softmax(x, axis=axis)
def _gelu(x):
    return jax.nn.gelu(x, approximate=True)
def _silu(x):
    return jax.nn.silu(x)
def _sigmoid(x):
    return jax.nn.sigmoid(x)
def _layernorm(x, axis=-1, eps=1e-5):
    m = jnp.mean(x, axis=axis, keepdims=True)
    v = jnp.var(x, axis=axis, keepdims=True)
    return (x - m) / jnp.sqrt(v + eps)
def _scatter_add(tgt, idx, src, axis=0):
    return tgt.at[idx].add(src)
def _segment_sum(src, seg, n):
    return jax.ops.segment_sum(src, seg, n)

kernel_name = 'mk_conv_seq_d2_conv_nchw1024_07f928'

def setup_inputs(seed: int = 0):
    np.random.seed(seed)
    _w = jnp.asarray
    def _rec_inputs():
        import jax
        import jax.numpy as jnp
        _gk = jax.random.key(seed)
        x = -0.0005207 + 1.001 * jax.random.normal(jax.random.fold_in(_gk, 1), (2, 1024, 32, 32), jnp.float32)
        return x
    x = _rec_inputs()
    def _L0_conv_setup():
        import jax, jax.numpy as jnp
        import numpy as np
        DIM = 32
        ED = DIM * DIM
        HID = ED * 4
        EPS = 1e-05

        def _ln(x, g, b):
            m = x.mean(axis=(-2, -1), keepdims=True)
            v = jnp.var(x, axis=(-2, -1), keepdims=True)
            return (x - m) * jax.lax.rsqrt(v + EPS) * g + b
        key = jax.random.key(seed)
        ks = jax.random.split(key, 10)
        b, s, d = (2, 1024, DIM)
        inp = {'x': jax.random.normal(ks[0], (b, s, d, d), dtype=jnp.float32), 'log_A': jax.random.normal(ks[1], (d,), dtype=jnp.float32) * 0.02, 'w_dt': jax.random.normal(ks[2], (d,), dtype=jnp.float32) / np.sqrt(d), 'b_dt': jnp.zeros((), dtype=jnp.float32), 'g_ssm': jnp.ones((d, d), dtype=jnp.float32), 'b_ssm': jnp.zeros((d, d), dtype=jnp.float32), 'g_ffn': jnp.ones((d, d), dtype=jnp.float32), 'b_ffn': jnp.zeros((d, d), dtype=jnp.float32), 'W1': jax.random.normal(ks[3], (ED, HID), dtype=jnp.float32) / np.sqrt(ED), 'bb1': jnp.zeros((HID,), dtype=jnp.float32), 'W2': jax.random.normal(ks[4], (HID, ED), dtype=jnp.float32) / np.sqrt(HID), 'bb2': jnp.zeros((ED,), dtype=jnp.float32)}
        return inp
    _L0_conv_all = _L0_conv_setup()
    _L0_conv_in = {k: v for k, v in _L0_conv_all.items() if k in ('log_A', 'w_dt', 'b_dt', 'g_ssm', 'b_ssm', 'g_ffn', 'b_ffn', 'W1', 'bb1', 'W2', 'bb2', )}
    del _L0_conv_all

    def _L1_conv_setup():
        import jax, jax.numpy as jnp
        import numpy as np
        import math
        B, CIN, CP, H, W = (16, 1024, 512, 32, 32)
        ORDER = 2
        GAMMA = 0.0001
        EPS = 1e-05

        def _rbf_kernel(t, p, g):
            b, c, h, w = t.shape
            n = c * h * w
            tf = t.reshape(b, n)
            pf = p.reshape(b, n)
            gf = g.reshape(b, n)
            beta = math.exp(-2.0 * GAMMA)
            alphas = [math.sqrt((2.0 * GAMMA) ** o / math.factorial(o) * beta) for o in range(ORDER + 1)]
            t_taylor = jnp.stack([jnp.float32(a) * tf ** o for o, a in enumerate(alphas)], axis=1)
            p_taylor = jnp.stack([jnp.float32(a) * pf ** o for o, a in enumerate(alphas)], axis=1)
            att = jnp.einsum('bkn,bn->bk', p_taylor, gf)
            out = jnp.einsum('bk,bkn->bn', att, t_taylor)
            return out.reshape(b, c, h, w)
        key = jax.random.key(seed)
        k = jax.random.split(key, 5)
        x = jax.random.normal(k[0], (B, CIN, H, W), dtype=jnp.float32)
        s_in = 1.0 / math.sqrt(CIN)
        s_p = 1.0 / math.sqrt(CP)
        Wt = jax.random.normal(k[1], (CP, CIN), dtype=jnp.float32) * s_in
        Wp = jax.random.normal(k[2], (CP, CIN), dtype=jnp.float32) * s_in
        Wg = jax.random.normal(k[3], (CP, CIN), dtype=jnp.float32) * s_in
        Wz = jax.random.normal(k[4], (CIN, CP), dtype=jnp.float32) * s_p
        gn_w = jnp.ones((CIN,), dtype=jnp.float32)
        gn_b = jnp.zeros((CIN,), dtype=jnp.float32)
        return {'x': x, 'Wt': Wt, 'Wp': Wp, 'Wg': Wg, 'Wz': Wz, 'gn_w': gn_w, 'gn_b': gn_b}
    _L1_conv_all = _L1_conv_setup()
    _L1_conv_in = {k: v for k, v in _L1_conv_all.items() if k in ('Wt', 'Wp', 'Wg', 'Wz', 'gn_w', 'gn_b', )}
    del _L1_conv_all

    return {
        "x": x,
        "L0_conv_log_A": _L0_conv_in["log_A"],
        "L0_conv_w_dt": _L0_conv_in["w_dt"],
        "L0_conv_b_dt": _L0_conv_in["b_dt"],
        "L0_conv_g_ssm": _L0_conv_in["g_ssm"],
        "L0_conv_b_ssm": _L0_conv_in["b_ssm"],
        "L0_conv_g_ffn": _L0_conv_in["g_ffn"],
        "L0_conv_b_ffn": _L0_conv_in["b_ffn"],
        "L0_conv_W1": _L0_conv_in["W1"],
        "L0_conv_bb1": _L0_conv_in["bb1"],
        "L0_conv_W2": _L0_conv_in["W2"],
        "L0_conv_bb2": _L0_conv_in["bb2"],
        "L1_conv_Wt": _L1_conv_in["Wt"],
        "L1_conv_Wp": _L1_conv_in["Wp"],
        "L1_conv_Wg": _L1_conv_in["Wg"],
        "L1_conv_Wz": _L1_conv_in["Wz"],
        "L1_conv_gn_w": _L1_conv_in["gn_w"],
        "L1_conv_gn_b": _L1_conv_in["gn_b"],
    }

def reference(x, L0_conv_log_A, L0_conv_w_dt, L0_conv_b_dt, L0_conv_g_ssm, L0_conv_b_ssm, L0_conv_g_ffn, L0_conv_b_ffn, L0_conv_W1, L0_conv_bb1, L0_conv_W2, L0_conv_bb2, L1_conv_Wt, L1_conv_Wp, L1_conv_Wg, L1_conv_Wz, L1_conv_gn_w, L1_conv_gn_b):
    import jax
    import jax.numpy as jnp
    def _L0_conv_ref(x, log_A, w_dt, b_dt, g_ssm, b_ssm, g_ffn, b_ffn, W1, bb1, W2, bb2):
        import jax, jax.numpy as jnp
        import numpy as np
        DIM = 32
        ED = DIM * DIM
        HID = ED * 4
        EPS = 1e-05

        def _ln(x, g, b):
            m = x.mean(axis=(-2, -1), keepdims=True)
            v = jnp.var(x, axis=(-2, -1), keepdims=True)
            return (x - m) * jax.lax.rsqrt(v + EPS) * g + b
        b, s, d, _ = x.shape
        xn = _ln(x, g_ssm, b_ssm)
        A_cont = -jnp.exp(log_A)
        dt = jax.nn.softplus(jnp.einsum('bsrc,c->bsr', xn, w_dt) + b_dt)
        log_a = dt * A_cont
        cs = jnp.cumsum(log_a, axis=1)
        log_M = cs[:, :, None, :] - cs[:, None, :, :]
        tmask = jnp.arange(s)[:, None] >= jnp.arange(s)[None, :]
        M = jnp.where(tmask[None, :, :, None], jnp.exp(log_M), 0.0)
        ssm_out = jnp.einsum('btjr,bjrc->btrc', M, xn) + x
        fn = _ln(ssm_out, g_ffn, b_ffn).reshape(b, s, d * d)
        h = jax.nn.gelu(fn @ W1 + bb1, approximate=False)
        y = (h @ W2 + bb2).reshape(b, s, d, d)
        return ssm_out + y

    def _L1_conv_ref(x, Wt, Wp, Wg, Wz, gn_w, gn_b):
        import jax, jax.numpy as jnp
        import numpy as np
        import math
        B, CIN, CP, H, W = (16, 1024, 512, 32, 32)
        ORDER = 2
        GAMMA = 0.0001
        EPS = 1e-05

        def _rbf_kernel(t, p, g):
            b, c, h, w = t.shape
            n = c * h * w
            tf = t.reshape(b, n)
            pf = p.reshape(b, n)
            gf = g.reshape(b, n)
            beta = math.exp(-2.0 * GAMMA)
            alphas = [math.sqrt((2.0 * GAMMA) ** o / math.factorial(o) * beta) for o in range(ORDER + 1)]
            t_taylor = jnp.stack([jnp.float32(a) * tf ** o for o, a in enumerate(alphas)], axis=1)
            p_taylor = jnp.stack([jnp.float32(a) * pf ** o for o, a in enumerate(alphas)], axis=1)
            att = jnp.einsum('bkn,bn->bk', p_taylor, gf)
            out = jnp.einsum('bk,bkn->bn', att, t_taylor)
            return out.reshape(b, c, h, w)
        t = jnp.einsum('oc,bchw->bohw', Wt, x)
        p = jnp.einsum('oc,bchw->bohw', Wp, x)
        g = jnp.einsum('oc,bchw->bohw', Wg, x)
        y = _rbf_kernel(t, p, g)
        z = jnp.einsum('oc,bchw->bohw', Wz, y)
        mu = jnp.mean(z, axis=(1, 2, 3), keepdims=True)
        var = jnp.mean((z - mu) ** 2, axis=(1, 2, 3), keepdims=True)
        zn = (z - mu) * jax.lax.rsqrt(var + EPS)
        zn = zn * gn_w[None, :, None, None] + gn_b[None, :, None, None]
        return zn + x

    def _gn(v, G=32, eps=1e-5):
        B_, C_, H_, W_ = v.shape
        g = v.reshape(B_, G, C_ // G, H_, W_)
        m = jnp.mean(g, axis=(2, 3, 4), keepdims=True)
        s = jnp.var(g, axis=(2, 3, 4), keepdims=True)
        return ((g - m) / jnp.sqrt(s + eps)).reshape(v.shape)

    def _ln_c(v, eps=1e-6):
        m = jnp.mean(v, axis=1, keepdims=True)
        s = jnp.var(v, axis=1, keepdims=True)
        return (v - m) / jnp.sqrt(s + eps)

    def _ln_t(v, eps=1e-5):
        m = jnp.mean(v, axis=-1, keepdims=True)
        s = jnp.var(v, axis=-1, keepdims=True)
        return (v - m) / jnp.sqrt(s + eps)

    def _to_tokens(v):
        B_, C_, H_, W_ = v.shape
        return v.reshape(B_, C_, H_ * W_).transpose(0, 2, 1)
    def _from_tokens(t, like):
        B_, C_, H_, W_ = like.shape
        return t.transpose(0, 2, 1).reshape(B_, C_, H_, W_)

    x = _L0_conv_ref(x, L0_conv_log_A, L0_conv_w_dt, L0_conv_b_dt, L0_conv_g_ssm, L0_conv_b_ssm, L0_conv_g_ffn, L0_conv_b_ffn, L0_conv_W1, L0_conv_bb1, L0_conv_W2, L0_conv_bb2)
    x = _L1_conv_ref(x, L1_conv_Wt, L1_conv_Wp, L1_conv_Wg, L1_conv_Wz, L1_conv_gn_w, L1_conv_gn_b)
    return x


_drawn_inputs = setup_inputs


def setup_inputs(seed=0):
    import zlib

    import numpy as np

    out = dict(_drawn_inputs(seed))
    spreads = {'L0_conv_g_ssm': (1.0, 0.2),
     'L0_conv_b_ssm': (0.0, 0.1),
     'L0_conv_g_ffn': (1.0, 0.2),
     'L0_conv_b_ffn': (0.0, 0.3),
     'L0_conv_bb1': (0.0, 0.305),
     'L0_conv_bb2': (0.0, 0.1),
     'L1_conv_gn_w': (1.0, 0.2),
     'L1_conv_gn_b': (0.0, 0.1)}
    factors = {'L0_conv_log_A': 8.0, 'L1_conv_Wt': 8.0, 'L1_conv_Wp': 8.0, 'L1_conv_Wg': 8.0}
    for name, (base, spread) in spreads.items():
        noise = np.random.default_rng([zlib.crc32(name.encode()), seed]).standard_normal(out[name].shape)
        drawn = base * np.exp(spread * noise) if base else spread * noise
        out[name] = jnp.asarray(drawn.astype(out[name].dtype))
    for name, factor in factors.items():
        out[name] = (out[name] * factor).astype(out[name].dtype)
    return out
```

```python
import math

import concourse.bass as bass
from concourse import mybir

F32 = mybir.dt.float32
F32R = mybir.dt.float32r
ACT = mybir.ActivationFunctionType
ALU = mybir.AluOpType
AX_X = mybir.AxisListType.X

P = 128
HALF = 512
B, S, ED, HID, CP = 2, 1024, 1024, 4096, 512
D = 32
ST, KT = S // P, ED // P
JB = 4
ROUNDS = HID // P // JB
OT = CP // P
RPT = P // D
LN_EPS = 1e-5
GAMMA = 1e-4
ALPHA2 = [(2.0 * GAMMA) ** k / math.factorial(k) * math.exp(-2.0 * GAMMA) for k in range(3)]

W1_SLABS = HID // P
SLABS = 2 * W1_SLABS + 4 * OT
TILES_FF = 2 * W1_SLABS
TILES_GP = TILES_FF + 4 * OT
TILES_T = TILES_GP + 2 * OT
TILES = TILES_T + 2 * ST
ROWS_Y = 1 + ST * ROUNDS
C_GS, C_BS, C_GF, C_BF, C_B1, C_GN, C_BN = 0, 8, 16, 24, 32, 64, 72
COLS = 80


def build(nc, x, slabs, w2, cols, bb2, w_dt, log_a, b_dt, consts, spread, out):
    K = 1024
    start = -(-nc.sbuf_base // 64) * 64

    def at(name, offset, shape, dt=F32):
        return nc.alloc_sbuf_tensor_at(name, shape, dt, offset=start + offset)

    acc = at("acc", 0, [P, ST, ED])
    act_hi = at("act_hi", 32 * K, [P, KT, S], F32R)
    act_lo = at("act_lo", 64 * K, [P, KT, S], F32R)
    dec = at("dec", 64 * K, [D, 3, S])
    hid_hi = at("hid_hi", 96 * K, [P, JB, S], F32R)
    hid_lo = at("hid_lo", 112 * K, [P, JB, S], F32R)
    xn = at("xn", 96 * K, [P, ST, ED])
    gsb = at("gsb", 96 * K, [P, OT, S])
    pg = at("pg", 112 * K, [P, 2, S])
    ppg = at("ppg", 120 * K, [P, S])
    w2_hi = at("w2_hi", 128 * K, [P, JB, ED], F32R)
    w2_lo = at("w2_lo", 144 * K, [P, JB, ED], F32R)
    hs = at("hs", 128 * K, [P, KT, S])
    zsb = at("zsb", 128 * K, [P, ST, ED])
    w1_hi = at("w1_hi", 160 * K, [P, 2, ED], F32R)
    w1_lo = at("w1_lo", 168 * K, [P, 2, ED], F32R)
    raw = at("raw", 176 * K, [P, 2, ED])
    part = at("part", 184 * K, [P, 4, HALF])
    bb2_b = at("bb2_b", 192 * K, [P, ED])
    spread_s = at("spread_s", 196 * K, [D, KT, P])
    o = 200 * K
    const_s = at("const_s", o, [P, P + KT * D]); o += 4 * (P + KT * D)
    ones = at("ones", o, [P, P]); o += 4 * P
    dtw = at("dtw", o, [P, KT, D]); o += 4 * KT * D
    col = at("col", o, [P, COLS]); o += 4 * COLS
    wcol = at("wcol", o, [P, 8]); o += 32
    drow = at("drow", o, [D, 8]); o += 32
    st6 = at("st6", o, [P, ST, 2, 6]); o += 48 * ST
    zst = at("zst", o, [P, 2 * ST, 6]); o += 24 * 2 * ST
    mv = at("mv", o, [P, ST, 2]); o += 8 * ST
    ve = at("ve", o, [P, ST]); o += 4 * ST
    rstd = at("rstd", o, [P, ST]); o += 4 * ST
    mhalf = at("mhalf", o, [P, 8]); o += 32
    gate = at("gate", o, [P, 8]); o += 32
    b1g = at("b1g", o, [P, 8]); o += 32
    gsum = at("gsum", o, [P, 2 * OT]); o += 8 * OT
    psum1 = at("psum1", o, [P, 2, OT]); o += 8 * OT
    s3 = at("s3", o, [P, 8]); o += 32
    alpha2 = at("alpha2", o, [P, 8]); o += 32
    coef = at("coef", o, [P, 8]); o += 32
    zmv = at("zmv", o, [P, 8]); o += 32
    zw = at("zw", o, [P, 8]); o += 32
    zscale = at("zscale", o, [P, ST]); o += 4 * ST
    zbias = at("zbias", o, [P, ST]); o += 4 * ST
    assert start + o <= nc.sbuf_usable_end
    ident = const_s[:, 0:P]
    mask = const_s[:, P:P + KT * D].rearrange("p (k r) -> p k r", k=KT)

    A = nc.alloc_psum_tensor("A", [P, 4, HALF], F32)
    C = nc.alloc_psum_tensor("C", [P, 4, HALF], F32)

    def pair(t, i):
        return t[:, 2 * (i % 2):2 * (i % 2) + 2, :]

    def flat(ap):
        return ap.rearrange("p a c -> p (a c)")

    sem = {}
    for n in ("const_in", "slab_in0", "slab_in1", "out_done", "ones_ready", "drow_ready", "negA_ready", "dtw_ready",
              "stats", "rows_ready", "ve_ready", "rstd_ready", "norm_ready", "tr_done", "xnT_ready", "dt_done",
              "abs_ready", "relu_ready", "exp_ready", "log_ready", "sp_ready", "decay_ready", "bc_done", "scanned",
              "back_done", "radd_done", "bb2_added", "fn_tr_done", "fn_parts", "fn_split",
              "w_hi_ready", "w_ready", "tileA", "gelu_parts", "hid_split", "tileC", "yadded",
              "x1_hi", "x1_split", "g_ready", "pg_ready", "p_used", "s3_ready", "tot_done", "coef_ready",
              "t_lin", "t_used", "y_parts", "y_split", "z_ready", "z_stats", "zmv_ready", "mu_done", "mu_ready",
              "zw_ready", "var_done", "zve_ready", "zrstd_ready", "zscale_ready", "zbias_ready", "zn_ready",
              "add_even", "add_odd", "dve_c", "alpha_ready", "b1_ready"):
        sem[n] = nc.alloc_semaphore(n)
    x_in = [nc.alloc_semaphore(f"x_in{i}") for i in range(ST)]
    slab_in = [sem["slab_in0"], sem["slab_in1"]]

    def slab_pos(g, j):
        return 8 * g + (0, 1, 4, 6)[j]

    W2_POS = (2, 3, 5, 7)

    def load_slab(sp, b, pos, slot, src):
        if not (isinstance(pos, int) and pos + SLABS * b < 2):
            sp.wait_ge(sem["w_ready"], pos + SLABS * b - 1)
        sp.dma_start(raw[:, slot, :], src).then_inc(slab_in[slot], 16)

    with nc.Block() as block:
        @block.sync
        def _(sp):
            for b in range(B):
                for st in range(ST):
                    if b:
                        sp.wait_ge(sem["add_odd" if st % 2 else "add_even"], (ST // 2) * (b - 1) + st // 2 + 1)
                    sp.dma_start(acc[:, st, :], x[b, st * P:(st + 1) * P, :]).then_inc(x_in[st], 16)
                    if b == 0 and st == 0:
                        for dst, src in ((const_s[:], consts), (col[:], cols), (spread_s[:].rearrange("r k p -> r (k p)"), spread),
                                         (bb2_b[:], bb2.partition_broadcast(P)),
                                         (drow[:, 0:1], log_a), (drow[:, 2:3], b_dt.partition_broadcast(D))):
                            sp.dma_start(dst, src).then_inc(sem["const_in"], 16)
                        for q in range(RPT):
                            sp.dma_start(wcol[q * D:(q + 1) * D, 0:1], w_dt).then_inc(sem["const_in"], 16)
                load_slab(sp, b, 0, 0, slabs[0])
                load_slab(sp, b, 1, 1, slabs[1])
                with sp.Fori(0, ROUNDS) as g:
                    p0 = 8 * g + 2
                    load_slab(sp, b, p0, 0, w2[JB * g])
                    load_slab(sp, b, p0 + 1, 1, w2[JB * g + 1])
                    load_slab(sp, b, p0 + 2, 0, slabs[JB * g + 2])
                    load_slab(sp, b, p0 + 3, 1, w2[JB * g + 2])
                    load_slab(sp, b, p0 + 4, 0, slabs[JB * g + 3])
                    load_slab(sp, b, p0 + 5, 1, w2[JB * g + 3])
                    load_slab(sp, b, p0 + 6, 0, slabs[JB * g + 4])
                    load_slab(sp, b, p0 + 7, 1, slabs[JB * g + 5])
                for m in range(W1_SLABS + 2, W1_SLABS + 4 * OT):
                    load_slab(sp, b, m + W1_SLABS, m % 2, slabs[m])
                for c in range(ST):
                    sp.wait_ge(sem["add_odd" if c % 2 else "add_even"], (ST // 2) * b + c // 2 + 1)
                    sp.dma_start(out[b, c * P:(c + 1) * P, :], zsb[:, c, :]).then_inc(sem["out_done"], 16)
            sp.wait_ge(sem["out_done"], 16 * ST * B)

        @block.gpsimd
        def _(pool):
            pool.memset(ones[:], 1.0).then_inc(sem["ones_ready"], 1)
            pool.memset(mhalf[:], -0.5).then_inc(sem["ones_ready"], 1)

            def split(b, pos, loads, slot, hi, lo, free):
                pool.wait_ge(slab_in[slot], loads * 16)
                for s, v in free:
                    pool.wait_ge(sem[s], v)
                nc.gpsimd.tensor_tensor(gate[:, 0:1], mhalf[:, 0:1], mhalf[:, 1:2], ALU.add)
                nc.gpsimd.tensor_copy(hi, raw[:, slot, :]).then_inc(sem["w_hi_ready"], 1)
                pool.wait_ge(sem["w_hi_ready"], pos + SLABS * b + 1)
                nc.gpsimd.tensor_tensor(lo, raw[:, slot, :], hi.bitcast(F32), ALU.subtract).then_inc(sem["w_ready"], 1)

            def w1(b, pos, loads, slot, ring, tiles):
                split(b, pos, loads, slot, w1_hi[:, ring, :], w1_lo[:, ring, :],
                      [("tileA", tiles)] if not (isinstance(tiles, int) and tiles <= 0) else [])

            def inv_std(n, eps):
                for st in range(ST):
                    pool.wait_ge(sem["stats"], n + st + 1)
                    nc.gpsimd.tensor_scalar(ve[:, st:st + 1], mv[:, st, 1:2], eps, None, ALU.add).then_inc(sem["ve_ready"], 1)
                    pool.wait_ge(sem["ve_ready"], n + st + 1)
                    nc.gpsimd.tensor_tensor(rstd[:, st:st + 1], ve[:, st:st + 1], mhalf[:, 0:1], ALU.pow)\
                        .then_inc(sem["rstd_ready"], 1)

            pool.wait_ge(sem["ones_ready"], 2)
            for b in range(B):
                inv_std(2 * ST * b, LN_EPS)
                base = TILES * b
                half = SLABS // 2 * b
                w1(b, 0, half + 1, 0, 0, base - 4)
                w1(b, 1, half + 1, 1, 1, base)
                inv_std(2 * ST * b + ST, LN_EPS)
                for st in range(ST):
                    pool.wait_ge(sem["norm_ready"], 2 * ST * b + ST + st + 1)
                    nc.gpsimd.tensor_tensor(acc[:, st, :], acc[:, st, :], bb2_b[:], ALU.add).then_inc(sem["bb2_added"], 1)
                with pool.Fori(0, ROUNDS) as g:
                    n0 = half + 4 * g + 2
                    u0 = base + 8 * g
                    w2_free = [("tileC", ROWS_Y * b + ST * g + 1)]
                    split(b, 8 * g + 2, n0, 0, w2_hi[:, 0, :], w2_lo[:, 0, :], w2_free)
                    split(b, 8 * g + 3, n0, 1, w2_hi[:, 1, :], w2_lo[:, 1, :], w2_free)
                    w1(b, 8 * g + 4, n0 + 1, 0, 0, u0 + 2)
                    split(b, 8 * g + 5, n0 + 1, 1, w2_hi[:, 2, :], w2_lo[:, 2, :], w2_free)
                    w1(b, 8 * g + 6, n0 + 2, 0, 1, u0 + 4)
                    split(b, 8 * g + 7, n0 + 2, 1, w2_hi[:, 3, :], w2_lo[:, 3, :], w2_free)
                    w1(b, 8 * g + 8, n0 + 3, 0, 0, u0 + 6)
                    w1(b, 8 * g + 9, n0 + 3, 1, 1, u0 + 8)
                for m in range(W1_SLABS + 2, W1_SLABS + 4 * OT):
                    pos = m + W1_SLABS
                    last = m - 2
                    tiles = 2 * (last + 1) if last < W1_SLABS + 3 * OT else TILES_T + 4 * (last - W1_SLABS - 3 * OT + 1)
                    w1(b, pos, half + pos // 2 + 1, pos % 2, m % 2, base + tiles)
                pool.wait_ge(sem["zve_ready"], b + 1)
                nc.gpsimd.tensor_tensor(zw[:, 3:4], zw[:, 2:3], mhalf[:, 0:1], ALU.pow).then_inc(sem["zrstd_ready"], 1)
                for c in range(1, ST, 2):
                    pool.wait_ge(sem["zn_ready"], ST * b + c + 1)
                    nc.gpsimd.tensor_tensor(zsb[:, c, :], zsb[:, c, :], acc[:, c, :], ALU.add).then_inc(sem["add_odd"], 1)

        @block.scalar
        def _(act):
            act.wait_ge(sem["const_in"], 16 * 10)
            nc.scalar.activation(drow[:, 1:2], drow[:, 0:1], ACT.Exp).then_inc(sem["drow_ready"], 1)
            act.wait_ge(sem["drow_ready"], 1)
            nc.scalar.activation(drow[:, 1:2], drow[:, 1:2], ACT.Copy, scale=-1.0).then_inc(sem["negA_ready"], 1)
            act.wait_ge(sem["negA_ready"], 1)
            act.wait_ge(sem["ones_ready"], 2)
            for b in range(B):
                if b:
                    act.wait_ge(sem["out_done"], 16 * ST * b)
                for k in range(KT):
                    act.wait_ge(sem["tr_done"], KT * b + k + 1)
                    nc.scalar.activation(hs[:, k, :], flat(pair(A, k)), ACT.Identity, bias=col[:, C_BS + k:C_BS + k + 1],
                                         scale=col[:, C_GS + k:C_GS + k + 1]).then_inc(sem["xnT_ready"], 1)
                act.wait_ge(sem["abs_ready"], b + 1)
                nc.scalar.activation(dec[:, 0, :], dec[:, 0, :], ACT.Exp).then_inc(sem["exp_ready"], 1)
                act.wait_ge(sem["exp_ready"], b + 1)
                nc.scalar.activation(dec[:, 0, :], dec[:, 0, :], ACT.Ln, bias=ones[0:D, 0:1]).then_inc(sem["log_ready"], 1)
                act.wait_ge(sem["sp_ready"], b + 1)
                nc.scalar.activation(dec[:, 2, :], dec[:, 1, :], ACT.Exp, scale=drow[:, 1:2]).then_inc(sem["decay_ready"], 1)
                for n in range(2):
                    for k in range(KT):
                        i = n * KT + k
                        act.wait_ge(sem["fn_tr_done"], 2 * KT * b + i + 1)
                        if i >= 4:
                            act.wait_ge(sem["fn_split"], 2 * KT * b + i - 3)
                        elif b:
                            act.wait_ge(sem["y_split"], 2 * OT * b)
                        c0, c1 = col[:, C_BF + k:C_BF + k + 1], col[:, C_GF + k:C_GF + k + 1]
                        nc.scalar.activation(part[:, i % 4, :], A[:, i % 4, :], ACT.Identity, bias=c0, scale=c1)
                        nc.scalar.activation(act_hi[:, k, n * HALF:(n + 1) * HALF], A[:, i % 4, :], ACT.Identity,
                                             bias=c0, scale=c1).then_inc(sem["fn_parts"], 1)
                act.wait_ge(sem["fn_split"], 2 * KT * (b + 1))

                def gelus(g, j, n, c1):
                    i = 2 * j + n
                    u = TILES_FF * b + 8 * g + i
                    act.wait_ge(sem["tileA"], TILES * b + 8 * g + i + 1)
                    if not isinstance(u, int) or u >= 4:
                        act.wait_ge(sem["hid_split"], u - 3)
                    if i == 0:
                        act.wait_ge(sem["tileC"], ROWS_Y * b + ST * g + 1)
                    nc.scalar.activation(part[:, i % 4, :], A[:, i % 4, :], ACT.Gelu, bias=c1)
                    nc.scalar.activation(hid_hi[:, j, n * HALF:(n + 1) * HALF], A[:, i % 4, :], ACT.Gelu, bias=c1)\
                        .then_inc(sem["gelu_parts"], 1)

                if b == 0:
                    act.wait_ge(sem["b1_ready"], 1)
                    for j in range(JB):
                        for n in range(2):
                            gelus(0, j, n, b1g[:, j:j + 1])
                with act.Fori(1 if b == 0 else 0, ROUNDS) as g:
                    act.wait_ge(sem["b1_ready"], ROUNDS * b + g + 1)
                    for j in range(JB):
                        for n in range(2):
                            gelus(g, j, n, b1g[:, j:j + 1])
                for st in range(ST):
                    act.wait_ge(sem["yadded"], ST * ROUNDS * (b + 1) - ST + st + 1)
                    nc.scalar.activation(act_hi[:, st, :], acc[:, st, :], ACT.Copy).then_inc(sem["x1_hi"], 1)
                for o in range(OT):
                    for n in range(2):
                        act.wait_ge(sem["tileA"], TILES * b + TILES_FF + 4 * o + n + 1)
                        nc.scalar.activation(gsb[:, o, n * HALF:(n + 1) * HALF], A[:, n, :], ACT.Copy,
                                             accum_out=gsum[:, 2 * o + n:2 * o + n + 1]).then_inc(sem["g_ready"], 1)
                for i in range(2 * OT):
                    act.wait_ge(sem["t_used"], 2 * OT * b + i + 1)
                    nc.scalar.activation(part[:, i % 4, :], part[:, i % 4, :], ACT.Identity, bias=coef[:, 0:1])\
                        .then_inc(sem["y_parts"], 1)
                    act.wait_ge(sem["y_parts"], 2 * (2 * OT * b + i) + 1)
                    nc.scalar.activation(hid_hi[:, i // 2, (i % 2) * HALF:(i % 2 + 1) * HALF], part[:, i % 4, :],
                                         ACT.Copy).then_inc(sem["y_parts"], 1)
                for i in range(2 * ST):
                    act.wait_ge(sem["tileA"], TILES * b + TILES_T + i + 1)
                    nc.scalar.activation(zsb[:, i // 2, (i % 2) * HALF:(i % 2 + 1) * HALF], A[:, i % 4, :], ACT.Copy)\
                        .then_inc(sem["z_ready"], 1)
                act.wait_ge(sem["zbias_ready"], b + 1)
                for c in range(ST):
                    nc.scalar.activation(zsb[:, c, :], zsb[:, c, :], ACT.Identity, bias=zbias[:, c:c + 1],
                                         scale=zscale[:, c:c + 1]).then_inc(sem["zn_ready"], 1)

        @block.vector
        def _(dve):
            chain = [0]

            def link(ins):
                chain[0] += 1
                ins.then_inc(sem["dve_c"], 1)
                dve.wait_ge(sem["dve_c"], chain[0])

            for k in range(3):
                nc.vector.memset(alpha2[:, k:k + 1], ALPHA2[k]).then_inc(sem["alpha_ready"], 1)
            dve.wait_ge(sem["const_in"], 16 * 10)
            nc.vector.tensor_scalar(dtw[:], mask, wcol[:, 0:1], None, ALU.mult).then_inc(sem["dtw_ready"], 1)
            dve.wait_ge(sem["alpha_ready"], 3)

            def row_stats(n, ready=None):
                for st in range(ST + 1):
                    if st < ST:
                        if ready:
                            ready(st)
                        for h in range(2):
                            i = nc.vector.bn_stats(st6[:, st, h, :], acc[:, st, h * HALF:(h + 1) * HALF])
                        i.then_inc(sem["rows_ready"], 1)
                    if st:
                        dve.wait_ge(sem["rows_ready"], n + st)
                        nc.vector.bn_aggr(mv[:, st - 1, :], st6[:, st - 1, :, :].rearrange("p a c -> p (a c)"))\
                            .then_inc(sem["stats"], 1)

            def normalise(n):
                for st in range(ST):
                    dve.wait_ge(sem["rstd_ready"], n + st + 1)
                    nc.vector.tensor_scalar(xn[:, st, :], acc[:, st, :], mv[:, st, 0:1], rstd[:, st:st + 1],
                                            ALU.subtract, ALU.mult).then_inc(sem["norm_ready"], 1)

            def split_part(i, name, v, dst):
                dve.wait_ge(sem[name], v)
                return nc.vector.tensor_tensor(dst[0], part[:, i % 4, :], dst[1].bitcast(F32), ALU.subtract)

            for b in range(B):
                n0 = 2 * ST * b
                row_stats(n0, lambda st: dve.wait_ge(x_in[st], 16 * (b + 1)))
                dve.wait_ge(sem["stats"], n0 + ST)
                normalise(n0)
                dve.wait_ge(sem["dt_done"], b + 1)
                V = flat(C[0:D, 0:2, :])
                nc.vector.tensor_scalar(dec[:, 0, :], V, drow[:, 2:3], 0.0, ALU.add, ALU.min)
                nc.vector.tensor_scalar(dec[:, 1, :], V, drow[:, 2:3], 0.0, ALU.add, ALU.max).then_inc(sem["relu_ready"], 1)
                dve.wait_ge(sem["relu_ready"], b + 1)
                nc.vector.tensor_tensor(dec[:, 0, :], dec[:, 0, :], dec[:, 1, :], ALU.subtract).then_inc(sem["abs_ready"], 1)
                dve.wait_ge(sem["log_ready"], b + 1)
                nc.vector.tensor_tensor(dec[:, 1, :], dec[:, 1, :], dec[:, 0, :], ALU.add).then_inc(sem["sp_ready"], 1)
                for k in range(KT + 1):
                    if k < KT:
                        dve.wait_ge(sem["bc_done"], KT * b + k + 1)
                        nc.vector.tensor_tensor_scan(hs[:, k, :], flat(pair(A, k)), hs[:, k, :], 0.0, ALU.mult, ALU.add)\
                            .then_inc(sem["scanned"], 1)
                    if k:
                        kk = k - 1
                        dve.wait_ge(sem["back_done"], KT * b + k)
                        cols_k = acc[:, :, kk * P:(kk + 1) * P]
                        nc.vector.tensor_tensor(cols_k, flat(pair(C, kk)).rearrange("p (s c) -> p s c", s=ST), cols_k, ALU.add)\
                            .then_inc(sem["radd_done"], 1)
                dve.wait_ge(sem["radd_done"], KT * (b + 1))
                row_stats(n0 + ST)
                dve.wait_ge(sem["stats"], n0 + 2 * ST)
                normalise(n0 + ST)
                for i in range(2 * KT):
                    n, k = i // KT, i % KT
                    cut = (slice(None), k, slice(n * HALF, (n + 1) * HALF))
                    split_part(i, "fn_parts", 2 * KT * b + i + 1, (act_lo[cut], act_hi[cut])).then_inc(sem["fn_split"], 1)
                dve.wait_ge(sem["bb2_added"], ST * (b + 1))

                def hid_parts(g):
                    for i in range(2 * JB):
                        cut = (slice(None), i // 2, slice((i % 2) * HALF, (i % 2 + 1) * HALF))
                        split_part(i, "gelu_parts", TILES_FF * b + 8 * g + i + 1, (hid_lo[cut], hid_hi[cut]))\
                            .then_inc(sem["hid_split"], 1)

                def round_bias(g):
                    nc.vector.tensor_scalar(b1g[:, 0:JB], col[:, bass.ds(C_B1 + JB * g, JB)], 0.0, None, ALU.add)\
                        .then_inc(sem["b1_ready"], 1)

                round_bias(0)

                def add_y(g, st):
                    dve.wait_ge(sem["tileC"], ROWS_Y * b + ST * g + st + 2)
                    nc.vector.tensor_tensor(acc[:, st, :], flat(pair(C, st)), acc[:, st, :], ALU.add)\
                        .then_inc(sem["yadded"], 1)

                def x1_part(st):
                    dve.wait_ge(sem["x1_hi"], ST * b + st + 1)
                    nc.vector.tensor_tensor(act_lo[:, st, :], acc[:, st, :], act_hi[:, st, :].bitcast(F32), ALU.subtract)\
                        .then_inc(sem["x1_split"], 1)

                with dve.Fori(0, ROUNDS - 1) as g:
                    hid_parts(g)
                    round_bias(g + 1)
                    for st in range(ST):
                        add_y(g, st)
                    dve.wait_ge(sem["yadded"], ST * ROUNDS * b + ST * g + ST)
                hid_parts(ROUNDS - 1)
                for st in range(ST):
                    add_y(ROUNDS - 1, st)
                    if st:
                        x1_part(st - 1)
                x1_part(ST - 1)
                for o in range(OT):
                    dve.wait_ge(sem["g_ready"], 2 * OT * b + 2 * o + 2)
                    dve.wait_ge(sem["tileA"], TILES * b + TILES_FF + 4 * o + 4)
                    pp = flat(A[:, 2:4, :])
                    nc.vector.tensor_tensor_reduce(out=pg[:, o % 2, :], in0=pp, in1=gsb[:, o, :], scale=1.0, scalar=0.0,
                                                   op0=ALU.mult, op1=ALU.add, accum_out=psum1[:, 0, o:o + 1])\
                        .then_inc(sem["pg_ready"], 1)
                    dve.wait_ge(sem["pg_ready"], OT * b + o + 1)
                    if o:
                        dve.wait_ge(sem["p_used"], OT * b + o)
                    nc.vector.tensor_tensor_reduce(out=ppg[:], in0=pp, in1=pg[:, o % 2, :], scale=1.0, scalar=0.0,
                                                   op0=ALU.mult, op1=ALU.add, accum_out=psum1[:, 1, o:o + 1])\
                        .then_inc(sem["p_used"], 1)
                dve.wait_ge(sem["p_used"], OT * (b + 1))
                link(nc.vector.reduce_sum(s3[:, 0:1], gsum[:], AX_X))
                nc.vector.reduce_sum(s3[:, 1:3], psum1[:], AX_X).then_inc(sem["s3_ready"], 1)
                dve.wait_ge(sem["tot_done"], b + 1)
                nc.vector.tensor_tensor(coef[:, 0:3], C[:, 0, 0:3], alpha2[:, 0:3], ALU.mult).then_inc(sem["coef_ready"], 1)
                dve.wait_ge(sem["coef_ready"], b + 1)
                for i in range(2 * OT + 1):
                    if i < 2 * OT:
                        dve.wait_ge(sem["tileA"], TILES * b + TILES_GP + i + 1)
                        if i >= 4:
                            dve.wait_ge(sem["y_split"], 2 * OT * b + i - 3)
                        nc.vector.tensor_scalar(part[:, i % 4, :], A[:, i % 4, :], coef[:, 2:3], coef[:, 1:2],
                                                ALU.mult, ALU.add).then_inc(sem["t_lin"], 1)
                        dve.wait_ge(sem["t_lin"], 2 * OT * b + i + 1)
                        nc.vector.tensor_tensor(part[:, i % 4, :], A[:, i % 4, :], part[:, i % 4, :], ALU.mult)\
                            .then_inc(sem["t_used"], 1)
                    if i:
                        h = i - 1
                        cut = (slice(None), h // 2, slice((h % 2) * HALF, (h % 2 + 1) * HALF))
                        split_part(h, "y_parts", 2 * (2 * OT * b + i), (hid_lo[cut], hid_hi[cut])).then_inc(sem["y_split"], 1)
                for i in range(2 * ST):
                    dve.wait_ge(sem["z_ready"], 2 * ST * b + i + 1)
                    nc.vector.bn_stats(zst[:, i, :], zsb[:, i // 2, (i % 2) * HALF:(i % 2 + 1) * HALF])\
                        .then_inc(sem["z_stats"], 1)
                dve.wait_ge(sem["z_stats"], 2 * ST * (b + 1))
                nc.vector.bn_aggr(zmv[:, 0:2], zst[:].rearrange("p a c -> p (a c)")).then_inc(sem["zmv_ready"], 1)
                dve.wait_ge(sem["zmv_ready"], b + 1)
                dve.wait_ge(sem["mu_done"], b + 1)
                link(nc.vector.tensor_scalar(zmv[:, 2:3], C[:, 1, 0:1], 1.0 / P, None, ALU.mult))
                link(nc.vector.tensor_tensor(zmv[:, 3:4], zmv[:, 0:1], zmv[:, 2:3], ALU.subtract))
                link(nc.vector.tensor_tensor(zmv[:, 4:5], zmv[:, 3:4], zmv[:, 3:4], ALU.mult))
                nc.vector.tensor_tensor(zw[:, 0:1], zmv[:, 4:5], zmv[:, 1:2], ALU.add).then_inc(sem["zw_ready"], 1)
                dve.wait_ge(sem["var_done"], b + 1)
                nc.vector.tensor_scalar(zw[:, 2:3], C[:, 2, 0:1], 1.0 / P, LN_EPS, ALU.mult, ALU.add)\
                    .then_inc(sem["zve_ready"], 1)
                dve.wait_ge(sem["zrstd_ready"], b + 1)
                nc.vector.tensor_scalar(zscale[:], col[:, C_GN:C_GN + ST], zw[:, 3:4], None, ALU.mult)\
                    .then_inc(sem["zscale_ready"], 1)
                dve.wait_ge(sem["zscale_ready"], b + 1)
                link(nc.vector.tensor_scalar(zbias[:], zscale[:], zmv[:, 2:3], -1.0, ALU.mult, ALU.mult))
                nc.vector.tensor_tensor(zbias[:], zbias[:], col[:, C_BN:C_BN + ST], ALU.add).then_inc(sem["zbias_ready"], 1)
                for c in range(0, ST, 2):
                    dve.wait_ge(sem["zn_ready"], ST * b + c + 1)
                    nc.vector.tensor_tensor(zsb[:, c, :], zsb[:, c, :], acc[:, c, :], ALU.add).then_inc(sem["add_even"], 1)

        @block.tensor
        def _(pe):
            def three(dst, hi, lo, rhs_hi, rhs_lo, first, last):
                nc.tensor.matmul(dst, hi, rhs_hi, start=first, stop=False)
                nc.tensor.matmul(dst, hi, rhs_lo, start=False, stop=False)
                return nc.tensor.matmul(dst, lo, rhs_hi, start=False, stop=last)

            def slab_tile(bank, ring, n, off=0, kn=KT, width=P, src=(act_hi, act_lo)):
                for k in range(kn):
                    c = slice(k * width + off, k * width + off + P)
                    r = slice(n * HALF, (n + 1) * HALF)
                    last = three(A[:, bank, :], w1_hi[:, ring, c], w1_lo[:, ring, c], src[0][:, k, r], src[1][:, k, r],
                                 k == 0, k == kn - 1)
                return last.then_inc(sem["tileA"], 1)

            pe.wait_ge(sem["const_in"], 16 * 10)
            pe.wait_ge(sem["dtw_ready"], 1)
            pe.wait_ge(sem["ones_ready"], 2)
            for b in range(B):
                TB = TILES * b
                pe.wait_ge(sem["norm_ready"], 2 * ST * b + ST)
                if b:
                    pe.wait_ge(sem["z_ready"], 2 * ST * b)
                    pe.wait_ge(sem["zve_ready"], b)
                for k in range(KT + 1):
                    if k < KT:
                        if k >= 2:
                            pe.wait_ge(sem["xnT_ready"], KT * b + k - 1)
                        dst = flat(pair(A, k))
                        for st in range(ST):
                            i = nc.tensor.transpose(dst[:, st * P:(st + 1) * P], xn[:, st, k * P:(k + 1) * P], ident)
                        i.then_inc(sem["tr_done"], 1)
                    if k:
                        pe.wait_ge(sem["xnT_ready"], KT * b + k)
                        for n in range(2):
                            i = nc.tensor.matmul(C[0:D, n, :], dtw[:, k - 1, :], hs[:, k - 1, n * HALF:(n + 1) * HALF],
                                                 start=k == 1, stop=k == KT)
                i.then_inc(sem["dt_done"], 1)
                pe.wait_ge(sem["decay_ready"], b + 1)
                for k in range(KT + 1):
                    if k < KT:
                        if k >= 2:
                            pe.wait_ge(sem["scanned"], KT * b + k - 1)
                        for n in range(2):
                            i = nc.tensor.matmul(pair(A, k)[:, n, :], spread_s[:, k, :], dec[:, 2, n * HALF:(n + 1) * HALF],
                                                 start=True, stop=True)
                        i.then_inc(sem["bc_done"], 1)
                    if k:
                        pe.wait_ge(sem["scanned"], KT * b + k)
                        if k >= 3:
                            pe.wait_ge(sem["radd_done"], KT * b + k - 2)
                        dst = flat(pair(C, k - 1))
                        for st in range(ST):
                            i = nc.tensor.transpose(dst[:, st * P:(st + 1) * P], hs[:, k - 1, st * P:(st + 1) * P], ident)
                        i.then_inc(sem["back_done"], 1)
                for n in range(2):
                    pe.wait_ge(sem["norm_ready"], 2 * ST * b + ST + (n + 1) * ST // 2)
                    for k in range(KT):
                        i = n * KT + k
                        if i >= 4:
                            pe.wait_ge(sem["fn_parts"], 2 * KT * b + i - 3)
                        for q in range(ST // 2):
                            ins = nc.tensor.transpose(A[:, i % 4, q * P:(q + 1) * P],
                                                      xn[:, n * ST // 2 + q, k * P:(k + 1) * P], ident)
                            if i == 0 and q == 0:
                                ins.then_inc(sem["tileC"], 1)
                        ins.then_inc(sem["fn_tr_done"], 1)
                pe.wait_ge(sem["fn_parts"], 2 * KT * (b + 1))
                pe.wait_ge(sem["radd_done"], KT * (b + 1))

                def ff_round(g):
                    for j in range(JB):
                        pe.wait_ge(sem["w_ready"], SLABS * b + slab_pos(g, j) + 1)
                        for n in range(2):
                            i = 2 * j + n
                            if not isinstance(g, int) or g or i >= 4:
                                pe.wait_ge(sem["gelu_parts"], TILES_FF * b + 8 * g + i - 3)
                            if isinstance(g, int) and g == 0 and j == 0:
                                pe.wait_ge(sem["fn_split"], 2 * KT * b + KT * (n + 1))
                            slab_tile(i % 4, j % 2, n)
                    for st in range(ST):
                        v = ST * ROUNDS * b + ST * g + st
                        if not isinstance(v, int) or v >= 2:
                            pe.wait_ge(sem["yadded"], v - 1)
                        for j in range(JB):
                            if st == 0:
                                pe.wait_ge(sem["w_ready"], SLABS * b + 8 * g + W2_POS[j] + 1)
                                pe.wait_ge(sem["hid_split"], TILES_FF * b + 8 * g + 2 * j + 2)
                            s = slice(st * P, (st + 1) * P)
                            for n in range(2):
                                r = slice(n * HALF, (n + 1) * HALF)
                                ins = three(pair(C, st)[:, n, :], hid_hi[:, j, s], hid_lo[:, j, s], w2_hi[:, j, r],
                                            w2_lo[:, j, r], j == 0, j == JB - 1)
                        ins.then_inc(sem["tileC"], 1)

                ff_round(0)
                with pe.Fori(1, ROUNDS) as g:
                    ff_round(g)

                def gp_tiles(o):
                    for w in range(2):
                        pe.wait_ge(sem["w_ready"], SLABS * b + 2 * W1_SLABS + 2 * o + w + 1)
                        if isinstance(o, int):
                            pe.wait_ge(sem["gelu_parts"], TILES_FF * (b + 1))
                        elif w == 0:
                            pe.wait_ge(sem["g_ready"], 2 * OT * b + 2 * o)
                        else:
                            pe.wait_ge(sem["p_used"], OT * b + o)
                        for n in range(2):
                            for k in range(KT):
                                if isinstance(o, int) and w == 0 and n == 0:
                                    pe.wait_ge(sem["x1_split"], ST * b + k + 1)
                                c = slice(k * P, (k + 1) * P)
                                r = slice(n * HALF, (n + 1) * HALF)
                                ins = three(A[:, 2 * w + n, :], w1_hi[:, w, c], w1_lo[:, w, c], act_hi[:, k, r],
                                            act_lo[:, k, r], k == 0, k == KT - 1)
                            ins.then_inc(sem["tileA"], 1)

                gp_tiles(0)
                with pe.Fori(1, OT) as o:
                    gp_tiles(o)

                def t_tile(o, i):
                    if i % 2 == 0:
                        pe.wait_ge(sem["w_ready"], SLABS * b + 2 * W1_SLABS + 2 * OT + o + 1)
                    slab_tile(i % 4, (i // 2) % 2, i % 2)

                pe.wait_ge(sem["g_ready"], 2 * OT * (b + 1))
                for i in range(2):
                    t_tile(0, i)
                pe.wait_ge(sem["s3_ready"], b + 1)
                nc.tensor.matmul(C[:, 0, 0:3], ones[:], s3[:, 0:3], start=True, stop=True).then_inc(sem["tot_done"], 1)
                pe.wait_ge(sem["p_used"], OT * (b + 1))
                for i in range(2, 2 * OT):
                    if i >= 4:
                        pe.wait_ge(sem["t_used"], 2 * OT * b + i - 3)
                    t_tile(i // 2, i)
                pe.wait_ge(sem["t_used"], 2 * OT * (b + 1))
                for i in range(2 * ST):
                    q, sub, n = i // 4, (i // 2) % 2, i % 2
                    if i % 4 == 0:
                        pe.wait_ge(sem["w_ready"], SLABS * b + 2 * W1_SLABS + 3 * OT + q + 1)
                    if i >= 4:
                        pe.wait_ge(sem["z_ready"], 2 * ST * b + i - 3)
                    for k in range(OT):
                        if i < 2:
                            pe.wait_ge(sem["y_split"], 2 * OT * b + 2 * k + n + 1)
                        c = slice(k * 2 * P + sub * P, k * 2 * P + (sub + 1) * P)
                        r = slice(n * HALF, (n + 1) * HALF)
                        ins = three(A[:, i % 4, :], w1_hi[:, q % 2, c], w1_lo[:, q % 2, c], hid_hi[:, k, r],
                                    hid_lo[:, k, r], k == 0, k == OT - 1)
                    ins.then_inc(sem["tileA"], 1)
                pe.wait_ge(sem["zmv_ready"], b + 1)
                nc.tensor.matmul(C[:, 1, 0:2], ones[:], zmv[:, 0:2], start=True, stop=True).then_inc(sem["mu_done"], 1)
                pe.wait_ge(sem["zw_ready"], b + 1)
                nc.tensor.matmul(C[:, 2, 0:1], ones[:], zw[:, 0:1], start=True, stop=True).then_inc(sem["var_done"], 1)


def kernel(**inputs):
    import numpy as np
    import concourse.bacc as bacc
    from concourse.bass_utils import run_bass_kernel_spmd

    v = {k: np.asarray(a) for k, a in inputs.items()}

    def slab(wt, width):
        r, c = wt.shape
        return wt.reshape(r // P, P, c // width, width).transpose(2, 1, 0, 3).reshape(c // width, P, r // P * width)

    wt, wp, wg, wz = (v["L1_conv_" + n].T for n in ("Wt", "Wp", "Wg", "Wz"))
    gp = np.stack([slab(wg, P), slab(wp, P)], axis=1).reshape(2 * OT, P, ED)
    by_tile = lambda a: a.reshape(-1, P).T
    eye = np.eye(P, dtype=np.float32)
    row_of = (np.arange(ED) // D)
    onehot = (row_of[:, None] == np.arange(D)[None, :]).astype(np.float32)
    arrays = {
        "x": v["x"].reshape(B, S, ED),
        "slabs": np.concatenate([slab(v["L0_conv_W1"], P), gp, slab(wt, P), slab(wz, 2 * P)], axis=0),
        "w2": v["L0_conv_W2"].reshape(W1_SLABS, P, ED),
        "cols": np.concatenate([by_tile(v[n].reshape(-1)) for n in (
            "L0_conv_g_ssm", "L0_conv_b_ssm", "L0_conv_g_ffn", "L0_conv_b_ffn", "L0_conv_bb1",
            "L1_conv_gn_w", "L1_conv_gn_b")], axis=1),
        "bb2": v["L0_conv_bb2"].reshape(ED),
        "w_dt": v["L0_conv_w_dt"].reshape(D, 1),
        "log_a": v["L0_conv_log_A"].reshape(D, 1),
        "b_dt": v["L0_conv_b_dt"].reshape(1),
        "consts": np.concatenate([eye, onehot.reshape(KT, P, D).transpose(1, 0, 2).reshape(P, KT * D)], axis=1),
        "spread": np.ascontiguousarray(onehot.T),
    }
    arrays = {k: np.ascontiguousarray(a) for k, a in arrays.items()}
    nc = bacc.Bacc("TRN2", target_bir_lowering=False, num_devices=1)
    args = [nc.dram_tensor(k, a.shape, mybir.dt.from_np(a.dtype), kind="ExternalInput").ap() for k, a in arrays.items()]
    out = nc.dram_tensor("out", (B, S, ED), F32, kind="ExternalOutput").ap()
    build(nc, *args, out)
    r = run_bass_kernel_spmd(nc, [arrays], core_ids=[0])
    return r.results[0]["out"].reshape(B, S, D, D)
```

```python
import math

import concourse.bass as bass
from concourse import mybir

F32 = mybir.dt.float32
F32R = mybir.dt.float32r
ACT = mybir.ActivationFunctionType
ALU = mybir.AluOpType
AX_X = mybir.AxisListType.X

P = 128
HALF = 512
B, S, ED, HID, CP = 2, 1024, 1024, 4096, 512
D = 32
ST, KT = S // P, ED // P
JB = 4
ROUNDS = HID // P // JB
OT = CP // P
RPT = P // D
LN_EPS = 1e-5
GAMMA = 1e-4
ALPHA2 = [(2.0 * GAMMA) ** k / math.factorial(k) * math.exp(-2.0 * GAMMA) for k in range(3)]

W1_SLABS = HID // P
SLABS = 2 * W1_SLABS + 4 * OT
TILES_FF = 2 * W1_SLABS
TILES_GP = TILES_FF + 4 * OT
TILES_T = TILES_GP + 2 * OT
TILES = TILES_T + 2 * ST
ROWS_Y = 1 + ST * ROUNDS
TR_AT = 9
CONST_DMAS = 5 + 2 * RPT
C_GS, C_BS, C_GF, C_BF, C_B1, C_GN, C_BN = 0, 8, 16, 24, 32, 64, 72
COLS = 80


def build(nc, x, slabs, w2, cols, bb2, w_dt, log_a, b_dt, consts, spread, out):
    K = 1024
    start = -(-nc.sbuf_base // 64) * 64

    def at(name, offset, shape, dt=F32):
        return nc.alloc_sbuf_tensor_at(name, shape, dt, offset=start + offset)

    acc = at("acc", 0, [P, ST, ED])
    act_hi = at("act_hi", 32 * K, [P, KT, S], F32R)
    act_lo = at("act_lo", 64 * K, [P, KT, S], F32R)
    xe = at("xe", 32 * K, [P, ST, ED])
    hs = at("hs", 64 * K, [P, KT, S])
    hid_hi = at("hid_hi", 96 * K, [P, JB, S], F32R)
    hid_lo = at("hid_lo", 112 * K, [P, JB, S], F32R)
    xr = at("xr", 96 * K, [P, ST, ED])
    xn = at("xn", 96 * K, [P, ST, ED])
    gsb = at("gsb", 96 * K, [P, OT, S])
    pg = at("pg", 112 * K, [P, 2, S])
    ppg = at("ppg", 120 * K, [P, S])
    w2_hi = at("w2_hi", 128 * K, [P, JB, ED], F32R)
    w2_lo = at("w2_lo", 144 * K, [P, JB, ED], F32R)
    zsb = at("zsb", 128 * K, [P, ST, ED])
    w1_hi = at("w1_hi", 160 * K, [P, 2, ED], F32R)
    w1_lo = at("w1_lo", 168 * K, [P, 2, ED], F32R)
    raw = at("raw", 176 * K, [P, 2, ED])
    part = at("part", 184 * K, [P, 4, HALF])
    dec = at("dec", 184 * K, [P, 2, S // 4])
    decay = at("decay", 186 * K, [P, S])
    bb2_b = at("bb2_b", 192 * K, [P, ED])
    spread_s = at("spread_s", 196 * K, [P, KT, P])
    o = 200 * K
    const_s = at("const_s", o, [P, P + KT * D]); o += 4 * (P + KT * D)
    ones = at("ones", o, [P, P]); o += 4 * P
    dtw = at("dtw", o, [P, KT, D]); o += 4 * KT * D
    col = at("col", o, [P, COLS]); o += 4 * COLS
    wcol = at("wcol", o, [P, 8]); o += 32
    drow = at("drow", o, [P, 8]); o += 32
    st6 = at("st6", o, [P, ST, 2, 6]); o += 48 * ST
    zst = at("zst", o, [P, 2 * ST, 6]); o += 24 * 2 * ST
    mv = at("mv", o, [P, ST, 2]); o += 8 * ST
    ve = at("ve", o, [P, ST]); o += 4 * ST
    rstd = at("rstd", o, [P, ST]); o += 4 * ST
    mhalf = at("mhalf", o, [P, 8]); o += 32
    b1g = at("b1g", o, [P, 8]); o += 32
    gsum = at("gsum", o, [P, 2 * OT]); o += 8 * OT
    psum1 = at("psum1", o, [P, 2, OT]); o += 8 * OT
    s3 = at("s3", o, [P, 8]); o += 32
    alpha2 = at("alpha2", o, [P, 8]); o += 32
    coef = at("coef", o, [P, 8]); o += 32
    zmv = at("zmv", o, [P, 8]); o += 32
    zw = at("zw", o, [P, 8]); o += 32
    zscale = at("zscale", o, [P, ST]); o += 4 * ST
    zbias = at("zbias", o, [P, ST]); o += 4 * ST
    assert start + o <= nc.sbuf_usable_end
    ident = const_s[:, 0:P]
    mask = const_s[:, P:P + KT * D].rearrange("p (k r) -> p k r", k=KT)

    A = nc.alloc_psum_tensor("A", [P, 4, HALF], F32)
    C = nc.alloc_psum_tensor("C", [P, 4, HALF], F32)

    def pair(t, i):
        return t[:, 2 * (i % 2):2 * (i % 2) + 2, :]

    def flat(ap):
        return ap.rearrange("p a c -> p (a c)")

    sem = {}
    for n in ("const_in", "slab_in0", "slab_in1", "out_done", "ones_ready", "drow_ready", "negA_ready", "dtw_ready",
              "stats", "rows_ready", "ve_ready", "rstd_ready", "norm_ready", "tr_done", "xnT_ready", "dt_done", "xr_in", "decay_zero", "fn_hi",
              "abs_ready", "relu_ready", "exp_ready", "log_ready", "sp_ready", "decay_ready", "bc_done", "scanned",
              "back_done", "radd_done", "bb2_added", "fn_tr_done", "fn_parts", "fn_split",
              "w_hi_ready", "w_ready", "tileA", "gelu_parts", "hid_split", "tileC", "yadded",
              "x1_hi", "x1_split", "g_ready", "pg_ready", "p_used", "s3_ready", "tot_done", "coef_ready",
              "t_lin", "t_used", "y_parts", "y_split", "z_ready", "z_stats", "zmv_ready", "mu_done", "mu_ready",
              "zw_ready", "var_done", "zve_ready", "zrstd_ready", "zscale_ready", "zbias_ready", "zn_ready",
              "add_dve", "add_pool", "dve_c", "alpha_ready", "b1_ready"):
        sem[n] = nc.alloc_semaphore(n)
    x_in = [nc.alloc_semaphore(f"x_in{i}") for i in range(ST)]
    slab_in = [sem["slab_in0"], sem["slab_in1"]]

    def slab_pos(g, j):
        return 8 * g + (0, 1, 4, 6)[j]

    W2_POS = (2, 3, 5, 7)

    def load_slab(sp, b, pos, slot, src):
        if not (isinstance(pos, int) and pos + SLABS * b < 2):
            sp.wait_ge(sem["w_ready"], pos + SLABS * b - 1)
        sp.dma_start(raw[:, slot, :], src).then_inc(slab_in[slot], 16)

    with nc.Block() as block:
        def added(b, c):
            if b < B - 1:
                return "add_pool", ST * b + c + 1
            return ("add_pool", ST * b + c // 2 + 1) if c % 2 else ("add_dve", c // 2 + 1)

        @block.sync
        def _(sp):
            def load_x(b, dst, sems):
                for st in range(ST):
                    sp.dma_start(dst[:, st, :], x[b, st * P:(st + 1) * P, :]).then_inc(sems[st % len(sems)], 16)

            load_x(0, xe, x_in)
            for dst, src in ((const_s[:], consts), (col[:], cols), (spread_s[:].rearrange("r k p -> r (k p)"), spread),
                             (bb2_b[:], bb2.partition_broadcast(P)), (drow[:, 2:3], b_dt.partition_broadcast(P))):
                sp.dma_start(dst, src).then_inc(sem["const_in"], 16)
            for q in range(P // D):
                sp.dma_start(wcol[q * D:(q + 1) * D, 0:1], w_dt).then_inc(sem["const_in"], 16)
                sp.dma_start(drow[q * D:(q + 1) * D, 0:1], log_a).then_inc(sem["const_in"], 16)
            load_slab(sp, 0, 0, 0, slabs[0])
            load_slab(sp, 0, 1, 1, slabs[1])
            load_x(0, xr, [sem["xr_in"]])
            for b in range(B):
                with sp.Fori(0, ROUNDS) as g:
                    p0 = 8 * g + 2
                    load_slab(sp, b, p0, 0, w2[JB * g])
                    load_slab(sp, b, p0 + 1, 1, w2[JB * g + 1])
                    load_slab(sp, b, p0 + 2, 0, slabs[JB * g + 2])
                    load_slab(sp, b, p0 + 3, 1, w2[JB * g + 2])
                    load_slab(sp, b, p0 + 4, 0, slabs[JB * g + 3])
                    load_slab(sp, b, p0 + 5, 1, w2[JB * g + 3])
                    load_slab(sp, b, p0 + 6, 0, slabs[JB * g + 4])
                    load_slab(sp, b, p0 + 7, 1, slabs[JB * g + 5])
                for m in range(W1_SLABS + 2, W1_SLABS + 4 * OT):
                    load_slab(sp, b, m + W1_SLABS, m % 2, slabs[m])
                    if b + 1 < B and m == W1_SLABS + 4 * OT - 2:
                        sp.wait_ge(sem["tileA"], TILES * b + TILES_T)
                        load_x(b + 1, xe, x_in)
                if b + 1 < B:
                    load_slab(sp, b + 1, 0, 0, slabs[0])
                    load_slab(sp, b + 1, 1, 1, slabs[1])
                    sp.wait_ge(sem["tileA"], TILES * (b + 1))
                    load_x(b + 1, xr, [sem["xr_in"]])
                for c in range(ST):
                    name, v = added(b, c)
                    sp.wait_ge(sem[name], v)
                    sp.dma_start(out[b, c * P:(c + 1) * P, :], zsb[:, c, :]).then_inc(sem["out_done"], 16)
            sp.wait_ge(sem["out_done"], 16 * ST * B)

        @block.gpsimd
        def _(pool):
            pool.memset(ones[:], 1.0).then_inc(sem["ones_ready"], 1)
            pool.memset(mhalf[:], -0.5).then_inc(sem["ones_ready"], 1)

            def low(b, pos, slot, hi, lo):
                pool.wait_ge(sem["w_hi_ready"], SLABS * b + pos + 1)
                nc.gpsimd.tensor_tensor(lo, raw[:, slot, :], hi.bitcast(F32), ALU.subtract).then_inc(sem["w_ready"], 1)

            def low1(b, pos, ring):
                low(b, pos, pos_slot(pos), w1_hi[:, ring, :], w1_lo[:, ring, :])

            def pos_slot(pos):
                return pos % 2

            def inv_std(n, eps):
                for st in range(ST):
                    pool.wait_ge(sem["stats"], n + st + 1)
                    nc.gpsimd.tensor_scalar(ve[:, st:st + 1], mv[:, st, 1:2], eps, None, ALU.add).then_inc(sem["ve_ready"], 1)
                    pool.wait_ge(sem["ve_ready"], n + st + 1)
                    nc.gpsimd.tensor_tensor(rstd[:, st:st + 1], ve[:, st:st + 1], mhalf[:, 0:1], ALU.pow)\
                        .then_inc(sem["rstd_ready"], 1)

            def z_out(b):
                pool.wait_ge(sem["zve_ready"], b + 1)
                nc.gpsimd.tensor_tensor(zw[:, 3:4], zw[:, 2:3], mhalf[:, 0:1], ALU.pow).then_inc(sem["zrstd_ready"], 1)
                for c in range(ST):
                    if added(b, c)[0] == "add_pool":
                        pool.wait_ge(sem["zn_ready"], ST * b + c + 1)
                        nc.gpsimd.tensor_tensor(zsb[:, c, :], zsb[:, c, :], acc[:, c, :], ALU.add)\
                            .then_inc(sem["add_pool"], 1)

            pool.wait_ge(sem["ones_ready"], 2)
            inv_std(0, LN_EPS)
            low1(0, 0, 0)
            low1(0, 1, 1)
            for b in range(B):
                if b:
                    pool.wait_ge(sem["y_split"], 2 * OT * b)
                nc.gpsimd.memset(decay[:], 0.0).then_inc(sem["decay_zero"], 1)
                if b:
                    z_out(b - 1)
                inv_std(2 * ST * b + ST, LN_EPS)
                for st in range(ST):
                    pool.wait_ge(sem["norm_ready"], 2 * ST * b + ST + st + 1)
                    nc.gpsimd.tensor_tensor(acc[:, st, :], acc[:, st, :], bb2_b[:], ALU.add).then_inc(sem["bb2_added"], 1)
                with pool.Fori(0, ROUNDS) as g:
                    low(b, 8 * g + 2, 0, w2_hi[:, 0, :], w2_lo[:, 0, :])
                    low(b, 8 * g + 3, 1, w2_hi[:, 1, :], w2_lo[:, 1, :])
                    low(b, 8 * g + 4, 0, w1_hi[:, 0, :], w1_lo[:, 0, :])
                    low(b, 8 * g + 5, 1, w2_hi[:, 2, :], w2_lo[:, 2, :])
                    low(b, 8 * g + 6, 0, w1_hi[:, 1, :], w1_lo[:, 1, :])
                    low(b, 8 * g + 7, 1, w2_hi[:, 3, :], w2_lo[:, 3, :])
                    low(b, 8 * g + 8, 0, w1_hi[:, 0, :], w1_lo[:, 0, :])
                    low(b, 8 * g + 9, 1, w1_hi[:, 1, :], w1_lo[:, 1, :])
                for m in range(W1_SLABS + 2, W1_SLABS + 4 * OT):
                    if b + 1 < B and m == W1_SLABS + 4 * OT - 2:
                        inv_std(2 * ST * (b + 1), LN_EPS)
                    low1(b, m + W1_SLABS, m % 2)
                if b + 1 < B:
                    low1(b + 1, 0, 0)
                    low1(b + 1, 1, 1)
            z_out(B - 1)

        @block.scalar
        def _(act):
            def high(b, pos, loads, slot, dst, free):
                act.wait_ge(slab_in[slot], 16 * loads)
                if free:
                    act.wait_ge(sem[free[0]], free[1])
                nc.scalar.activation(dst, raw[:, slot, :], ACT.Copy).then_inc(sem["w_hi_ready"], 1)

            def high1(b, m):
                pos = m if m < 2 else m + W1_SLABS
                last = m - 2 if m >= 2 else m + W1_SLABS + 4 * OT - 2
                done = 2 * (last + 1) if last < W1_SLABS + 3 * OT else TILES_T + 4 * (last - W1_SLABS - 3 * OT + 1)
                done += TILES * (b if m >= 2 else b - 1)
                high(b, pos, SLABS // 2 * b + pos // 2 + 1, pos % 2, w1_hi[:, m % 2, :], ("tileA", done) if done > 0 else None)

            def transposed(b, h):
                k, n = h // 2, h % 2
                act.wait_ge(sem["tr_done"], 2 * KT * b + h + 1)
                nc.scalar.activation(hs[:, k, n * HALF:(n + 1) * HALF], C[:, h % 3, :], ACT.Identity,
                                     bias=col[:, C_BS + k:C_BS + k + 1], scale=col[:, C_GS + k:C_GS + k + 1])\
                    .then_inc(sem["xnT_ready"], 1)

            def z_norm(b):
                act.wait_ge(sem["zbias_ready"], b + 1)
                for c in range(ST):
                    nc.scalar.activation(zsb[:, c, :], zsb[:, c, :], ACT.Identity, bias=zbias[:, c:c + 1],
                                         scale=zscale[:, c:c + 1]).then_inc(sem["zn_ready"], 1)

            act.wait_ge(sem["const_in"], 16 * CONST_DMAS)
            nc.scalar.activation(drow[:, 1:2], drow[:, 0:1], ACT.Exp).then_inc(sem["drow_ready"], 1)
            act.wait_ge(sem["drow_ready"], 1)
            nc.scalar.activation(drow[:, 3:4], drow[:, 1:2], ACT.Copy, scale=-1.0).then_inc(sem["negA_ready"], 1)
            act.wait_ge(sem["negA_ready"], 1)
            act.wait_ge(sem["ones_ready"], 2)
            for h in range(2 * KT):
                transposed(0, h)
            high1(0, 0)
            high1(0, 1)
            for b in range(B):
                act.wait_ge(sem["abs_ready"], b + 1)
                nc.scalar.activation(dec[:, 0, :], dec[:, 0, :], ACT.Exp).then_inc(sem["exp_ready"], 1)
                act.wait_ge(sem["exp_ready"], b + 1)
                nc.scalar.activation(dec[:, 0, :], dec[:, 0, :], ACT.Ln, bias=ones[:, 0:1]).then_inc(sem["log_ready"], 1)
                act.wait_ge(sem["sp_ready"], b + 1)
                act.wait_ge(sem["decay_zero"], b + 1)
                for j in range(4):
                    q = slice(j * D, (j + 1) * D)
                    nc.scalar.activation(decay[q, j * S // 4:(j + 1) * S // 4], dec[q, 1, :], ACT.Exp, scale=drow[q, 3:4])\
                        .then_inc(sem["decay_ready"], 1)
                if b:
                    z_norm(b - 1)
                for i in range(2 * KT):
                    k = i % KT
                    act.wait_ge(sem["fn_tr_done"], 2 * KT * b + i + 1)
                    if i >= 4:
                        act.wait_ge(sem["fn_split"], 2 * KT * b + i - 3)
                    nc.scalar.activation(part[:, i % 4, :], A[:, i % 4, :], ACT.Identity, bias=col[:, C_BF + k:C_BF + k + 1],
                                         scale=col[:, C_GF + k:C_GF + k + 1]).then_inc(sem["fn_parts"], 1)
                if b:
                    act.wait_ge(sem["out_done"], 16 * ST * b)
                act.wait_ge(sem["fn_split"], 2 * KT * (b + 1))

                def gelus(g, j):
                    for n in range(2):
                        i = 2 * j + n
                        u = TILES_FF * b + 8 * g + i
                        act.wait_ge(sem["tileA"], TILES * b + 8 * g + i + 1)
                        if not isinstance(u, int) or u >= 4:
                            act.wait_ge(sem["hid_split"], u - 3)
                        nc.scalar.activation(part[:, i % 4, :], A[:, i % 4, :], ACT.Gelu, bias=b1g[:, j:j + 1])
                        nc.scalar.activation(hid_hi[:, j, n * HALF:(n + 1) * HALF], A[:, i % 4, :], ACT.Gelu,
                                             bias=b1g[:, j:j + 1]).then_inc(sem["gelu_parts"], 1)

                def ff_round(g):
                    n0 = SLABS // 2 * b + 4 * g + 2
                    u0 = TILES * b + 8 * g
                    last = ("tileC", ROWS_Y * b + ST * g + 1)
                    high(b, 8 * g + 2, n0, 0, w2_hi[:, 0, :], last)
                    high(b, 8 * g + 3, n0, 1, w2_hi[:, 1, :], None)
                    act.wait_ge(sem["b1_ready"], ROUNDS * b + g + 1)
                    gelus(g, 0)
                    high(b, 8 * g + 4, n0 + 1, 0, w1_hi[:, 0, :], ("tileA", u0 + 2))
                    high(b, 8 * g + 5, n0 + 1, 1, w2_hi[:, 2, :], None)
                    gelus(g, 1)
                    high(b, 8 * g + 6, n0 + 2, 0, w1_hi[:, 1, :], ("tileA", u0 + 4))
                    high(b, 8 * g + 7, n0 + 2, 1, w2_hi[:, 3, :], None)
                    gelus(g, 2)
                    gelus(g, 3)
                    high(b, 8 * g + 8, n0 + 3, 0, w1_hi[:, 0, :], ("tileA", u0 + 6))
                    high(b, 8 * g + 9, n0 + 3, 1, w1_hi[:, 1, :], ("tileA", u0 + 8))

                if b == 0:
                    ff_round(0)
                with act.Fori(1 if b == 0 else 0, ROUNDS) as g:
                    ff_round(g)
                for st in range(ST):
                    act.wait_ge(sem["yadded"], ST * ROUNDS * (b + 1) - ST + st + 1)
                    nc.scalar.activation(act_hi[:, st, :], acc[:, st, :], ACT.Copy).then_inc(sem["x1_hi"], 1)
                act.wait_ge(sem["tileC"], ROWS_Y * (b + 1))
                for o in range(OT):
                    for n in range(2):
                        act.wait_ge(sem["tileA"], TILES * b + TILES_FF + 4 * o + n + 1)
                        nc.scalar.activation(gsb[:, o, n * HALF:(n + 1) * HALF], A[:, n, :], ACT.Copy,
                                             accum_out=gsum[:, 2 * o + n:2 * o + n + 1]).then_inc(sem["g_ready"], 1)
                    high1(b, W1_SLABS + 2 * o + 2)
                    high1(b, W1_SLABS + 2 * o + 3)
                for i in range(2 * OT):
                    act.wait_ge(sem["t_used"], 2 * OT * b + i + 1)
                    nc.scalar.activation(part[:, i % 4, :], part[:, i % 4, :], ACT.Identity, bias=coef[:, 0:1])\
                        .then_inc(sem["y_parts"], 1)
                    act.wait_ge(sem["y_parts"], 2 * (2 * OT * b + i) + 1)
                    nc.scalar.activation(hid_hi[:, i // 2, (i % 2) * HALF:(i % 2 + 1) * HALF], part[:, i % 4, :],
                                         ACT.Copy).then_inc(sem["y_parts"], 1)
                    if i % 2:
                        high1(b, W1_SLABS + 2 * OT + 2 + i // 2)
                for i in range(2 * ST):
                    act.wait_ge(sem["tileA"], TILES * b + TILES_T + i + 1)
                    nc.scalar.activation(zsb[:, i // 2, (i % 2) * HALF:(i % 2 + 1) * HALF], A[:, i % 4, :], ACT.Copy)\
                        .then_inc(sem["z_ready"], 1)
                    if b + 1 < B and i >= TR_AT:
                        transposed(b + 1, 2 * (i - TR_AT))
                        transposed(b + 1, 2 * (i - TR_AT) + 1)
                    if i % 4 == 3 and i < 8:
                        high1(b, W1_SLABS + 3 * OT + 2 + i // 4)
                    elif i % 4 == 3 and b + 1 < B:
                        high1(b + 1, i // 4 - 2)
                if b + 1 < B:
                    for h in range(2 * (2 * ST - TR_AT), 2 * KT):
                        transposed(b + 1, h)
            z_norm(B - 1)

        @block.vector
        def _(dve):
            chain = [0]

            def link(ins):
                chain[0] += 1
                ins.then_inc(sem["dve_c"], 1)
                dve.wait_ge(sem["dve_c"], chain[0])

            for k in range(3):
                nc.vector.memset(alpha2[:, k:k + 1], ALPHA2[k]).then_inc(sem["alpha_ready"], 1)
            dve.wait_ge(sem["const_in"], 16 * CONST_DMAS)
            nc.vector.tensor_scalar(dtw[:], mask, wcol[:, 0:1], None, ALU.mult).then_inc(sem["dtw_ready"], 1)
            dve.wait_ge(sem["alpha_ready"], 3)

            def normalise(n, st, src, dst):
                dve.wait_ge(sem["rstd_ready"], n + st + 1)
                nc.vector.tensor_scalar(dst[:, st, :], src[:, st, :], mv[:, st, 0:1], rstd[:, st:st + 1],
                                        ALU.subtract, ALU.mult).then_inc(sem["norm_ready"], 1)

            def split_part(i, name, v, dst):
                dve.wait_ge(sem[name], v)
                return nc.vector.tensor_tensor(dst[0], part[:, i % 4, :], dst[1].bitcast(F32), ALU.subtract)

            def minus_abs(b):
                dve.wait_ge(sem["dt_done"], b + 1)
                V = C[:, 3, 0:S // 4]
                nc.vector.tensor_scalar(dec[:, 0, :], V, drow[:, 2:3], 0.0, ALU.add, ALU.min)
                nc.vector.tensor_scalar(dec[:, 1, :], V, drow[:, 2:3], 0.0, ALU.add, ALU.max).then_inc(sem["relu_ready"], 1)
                dve.wait_ge(sem["relu_ready"], b + 1)
                nc.vector.tensor_tensor(dec[:, 0, :], dec[:, 0, :], dec[:, 1, :], ALU.subtract).then_inc(sem["abs_ready"], 1)

            def tile_stats(n, st, src):
                for h in range(2):
                    i = nc.vector.bn_stats(st6[:, st, h, :], src[:, st, h * HALF:(h + 1) * HALF])
                i.then_inc(sem["rows_ready"], 1)

            def tile_mv(n, st):
                dve.wait_ge(sem["rows_ready"], n + st + 1)
                nc.vector.bn_aggr(mv[:, st, :], st6[:, st, :, :].rearrange("p a c -> p (a c)")).then_inc(sem["stats"], 1)

            def x_stats(b, st):
                dve.wait_ge(x_in[st], 16 * (b + 1))
                tile_stats(2 * ST * b, st, xe)
                if st:
                    tile_mv(2 * ST * b, st - 1)

            for st in range(ST):
                x_stats(0, st)
            tile_mv(0, ST - 1)
            for st in range(ST):
                normalise(0, st, xe, xe)
            minus_abs(0)
            for b in range(B):
                n0 = 2 * ST * b
                dve.wait_ge(sem["log_ready"], b + 1)
                nc.vector.tensor_tensor(dec[:, 1, :], dec[:, 1, :], dec[:, 0, :], ALU.add).then_inc(sem["sp_ready"], 1)
                def residual(k):
                    dve.wait_ge(sem["back_done"], KT * b + k + 1)
                    c = slice(k * P, (k + 1) * P)
                    nc.vector.tensor_tensor(acc[:, :, c], flat(pair(C, k)).rearrange("p (s c) -> p s c", s=ST),
                                            xr[:, :, c], ALU.add).then_inc(sem["radd_done"], 1)

                lag = 2 if b else 1
                for k in range(KT + lag):
                    if k < KT:
                        dve.wait_ge(sem["bc_done"], KT * b + k + 1)
                        nc.vector.tensor_tensor_scan(hs[:, k, :], flat(pair(A, k)), hs[:, k, :], 0.0, ALU.mult, ALU.add)\
                            .then_inc(sem["scanned"], 1)
                    if k == lag:
                        dve.wait_ge(sem["xr_in"], 16 * ST * (b + 1))
                        if b:
                            dve.wait_ge(sem["add_pool"], ST * b)
                    if k >= lag:
                        residual(k - lag)
                dve.wait_ge(sem["radd_done"], KT * (b + 1))
                for st in range(ST):
                    tile_stats(n0 + ST, st, acc)
                    if st:
                        tile_mv(n0 + ST, st - 1)
                    if st >= 3:
                        normalise(n0 + ST, st - 3, acc, xn)
                tile_mv(n0 + ST, ST - 1)
                for st in range(ST - 3, ST):
                    normalise(n0 + ST, st, acc, xn)
                for i in range(2 * KT + 1):
                    if i < 2 * KT:
                        cut = (slice(None), i % KT, slice(i // KT * HALF, (i // KT + 1) * HALF))
                        dve.wait_ge(sem["fn_parts"], 2 * KT * b + i + 1)
                        nc.vector.tensor_copy(act_hi[cut], part[:, i % 4, :]).then_inc(sem["fn_hi"], 1)
                    if i:
                        h = i - 1
                        cut = (slice(None), h % KT, slice(h // KT * HALF, (h // KT + 1) * HALF))
                        split_part(h, "fn_hi", 2 * KT * b + h + 1, (act_lo[cut], act_hi[cut])).then_inc(sem["fn_split"], 1)
                dve.wait_ge(sem["bb2_added"], ST * (b + 1))

                def hid_parts(g):
                    for i in range(2 * JB):
                        cut = (slice(None), i // 2, slice((i % 2) * HALF, (i % 2 + 1) * HALF))
                        split_part(i, "gelu_parts", TILES_FF * b + 8 * g + i + 1, (hid_lo[cut], hid_hi[cut]))\
                            .then_inc(sem["hid_split"], 1)

                def round_bias(g):
                    nc.vector.tensor_scalar(b1g[:, 0:JB], col[:, bass.ds(C_B1 + JB * g, JB)], 0.0, None, ALU.add)\
                        .then_inc(sem["b1_ready"], 1)

                round_bias(0)

                def add_y(g, st):
                    dve.wait_ge(sem["tileC"], ROWS_Y * b + ST * g + st + 2)
                    nc.vector.tensor_tensor(acc[:, st, :], flat(pair(C, st)), acc[:, st, :], ALU.add)\
                        .then_inc(sem["yadded"], 1)

                def x1_part(st):
                    dve.wait_ge(sem["x1_hi"], ST * b + st + 1)
                    nc.vector.tensor_tensor(act_lo[:, st, :], acc[:, st, :], act_hi[:, st, :].bitcast(F32), ALU.subtract)\
                        .then_inc(sem["x1_split"], 1)

                with dve.Fori(0, ROUNDS - 1) as g:
                    hid_parts(g)
                    round_bias(g + 1)
                    for st in range(ST):
                        add_y(g, st)
                    dve.wait_ge(sem["yadded"], ST * ROUNDS * b + ST * g + ST)
                hid_parts(ROUNDS - 1)
                for st in range(ST):
                    add_y(ROUNDS - 1, st)
                    if st:
                        x1_part(st - 1)
                x1_part(ST - 1)
                for o in range(OT):
                    dve.wait_ge(sem["g_ready"], 2 * OT * b + 2 * o + 2)
                    dve.wait_ge(sem["tileA"], TILES * b + TILES_FF + 4 * o + 4)
                    pp = flat(A[:, 2:4, :])
                    nc.vector.tensor_tensor_reduce(out=pg[:, o % 2, :], in0=pp, in1=gsb[:, o, :], scale=1.0, scalar=0.0,
                                                   op0=ALU.mult, op1=ALU.add, accum_out=psum1[:, 0, o:o + 1])\
                        .then_inc(sem["pg_ready"], 1)
                    dve.wait_ge(sem["pg_ready"], OT * b + o + 1)
                    if o:
                        dve.wait_ge(sem["p_used"], OT * b + o)
                    nc.vector.tensor_tensor_reduce(out=ppg[:], in0=pp, in1=pg[:, o % 2, :], scale=1.0, scalar=0.0,
                                                   op0=ALU.mult, op1=ALU.add, accum_out=psum1[:, 1, o:o + 1])\
                        .then_inc(sem["p_used"], 1)
                dve.wait_ge(sem["p_used"], OT * (b + 1))
                link(nc.vector.reduce_sum(s3[:, 0:1], gsum[:], AX_X))
                nc.vector.reduce_sum(s3[:, 1:3], psum1[:], AX_X).then_inc(sem["s3_ready"], 1)
                dve.wait_ge(sem["tot_done"], b + 1)
                nc.vector.tensor_tensor(coef[:, 0:3], C[:, 0, 0:3], alpha2[:, 0:3], ALU.mult).then_inc(sem["coef_ready"], 1)
                dve.wait_ge(sem["coef_ready"], b + 1)
                for i in range(2 * OT + 1):
                    if i < 2 * OT:
                        dve.wait_ge(sem["tileA"], TILES * b + TILES_GP + i + 1)
                        if i >= 4:
                            dve.wait_ge(sem["y_split"], 2 * OT * b + i - 3)
                        nc.vector.tensor_scalar(part[:, i % 4, :], A[:, i % 4, :], coef[:, 2:3], coef[:, 1:2],
                                                ALU.mult, ALU.add).then_inc(sem["t_lin"], 1)
                        dve.wait_ge(sem["t_lin"], 2 * OT * b + i + 1)
                        nc.vector.tensor_tensor(part[:, i % 4, :], A[:, i % 4, :], part[:, i % 4, :], ALU.mult)\
                            .then_inc(sem["t_used"], 1)
                    if i:
                        h = i - 1
                        cut = (slice(None), h // 2, slice((h % 2) * HALF, (h % 2 + 1) * HALF))
                        split_part(h, "y_parts", 2 * (2 * OT * b + i), (hid_lo[cut], hid_hi[cut])).then_inc(sem["y_split"], 1)
                for i in range(2 * ST):
                    dve.wait_ge(sem["z_ready"], 2 * ST * b + i + 1)
                    nc.vector.bn_stats(zst[:, i, :], zsb[:, i // 2, (i % 2) * HALF:(i % 2 + 1) * HALF])\
                        .then_inc(sem["z_stats"], 1)
                    if b + 1 < B:
                        n1 = 2 * ST * (b + 1)
                        if 1 <= i <= 4:
                            x_stats(b + 1, 2 * i - 2)
                            x_stats(b + 1, 2 * i - 1)
                        if i == 4:
                            tile_mv(n1, ST - 1)
                            for st in range(ST):
                                normalise(n1, st, xe, xe)
                dve.wait_ge(sem["z_stats"], 2 * ST * (b + 1))
                nc.vector.bn_aggr(zmv[:, 0:2], zst[:].rearrange("p a c -> p (a c)")).then_inc(sem["zmv_ready"], 1)
                dve.wait_ge(sem["zmv_ready"], b + 1)
                dve.wait_ge(sem["mu_done"], b + 1)
                link(nc.vector.tensor_scalar(zmv[:, 2:3], A[:, 3, 0:1], 1.0 / P, None, ALU.mult))
                link(nc.vector.tensor_tensor(zmv[:, 3:4], zmv[:, 0:1], zmv[:, 2:3], ALU.subtract))
                link(nc.vector.tensor_tensor(zmv[:, 4:5], zmv[:, 3:4], zmv[:, 3:4], ALU.mult))
                nc.vector.tensor_tensor(zw[:, 0:1], zmv[:, 4:5], zmv[:, 1:2], ALU.add).then_inc(sem["zw_ready"], 1)
                if b + 1 < B:
                    minus_abs(b + 1)
                dve.wait_ge(sem["var_done"], b + 1)
                nc.vector.tensor_scalar(zw[:, 2:3], A[:, 3, 8:9], 1.0 / P, LN_EPS, ALU.mult, ALU.add)\
                    .then_inc(sem["zve_ready"], 1)
                dve.wait_ge(sem["zrstd_ready"], b + 1)
                nc.vector.tensor_scalar(zscale[:], col[:, C_GN:C_GN + ST], zw[:, 3:4], None, ALU.mult)\
                    .then_inc(sem["zscale_ready"], 1)
                dve.wait_ge(sem["zscale_ready"], b + 1)
                link(nc.vector.tensor_scalar(zbias[:], zscale[:], zmv[:, 2:3], -1.0, ALU.mult, ALU.mult))
                nc.vector.tensor_tensor(zbias[:], zbias[:], col[:, C_BN:C_BN + ST], ALU.add).then_inc(sem["zbias_ready"], 1)
            for c in range(ST):
                if added(B - 1, c)[0] == "add_dve":
                    dve.wait_ge(sem["zn_ready"], ST * (B - 1) + c + 1)
                    nc.vector.tensor_tensor(zsb[:, c, :], zsb[:, c, :], acc[:, c, :], ALU.add).then_inc(sem["add_dve"], 1)

        @block.tensor
        def _(pe):
            def three(dst, hi, lo, rhs_hi, rhs_lo, first, last):
                nc.tensor.matmul(dst, hi, rhs_hi, start=first, stop=False)
                nc.tensor.matmul(dst, hi, rhs_lo, start=False, stop=False)
                return nc.tensor.matmul(dst, lo, rhs_hi, start=False, stop=last)

            def slab_tile(bank, ring, n, off=0, kn=KT, width=P, src=(act_hi, act_lo)):
                for k in range(kn):
                    c = slice(k * width + off, k * width + off + P)
                    r = slice(n * HALF, (n + 1) * HALF)
                    last = three(A[:, bank, :], w1_hi[:, ring, c], w1_lo[:, ring, c], src[0][:, k, r], src[1][:, k, r],
                                 k == 0, k == kn - 1)
                return last.then_inc(sem["tileA"], 1)

            pe.wait_ge(sem["const_in"], 16 * CONST_DMAS)
            pe.wait_ge(sem["dtw_ready"], 1)
            pe.wait_ge(sem["ones_ready"], 2)

            def transpose_x(b, k):
                if k == 0:
                    pe.wait_ge(sem["norm_ready"], 2 * ST * b + ST)
                for n in range(2):
                    h = 2 * k + n
                    if h >= 3:
                        pe.wait_ge(sem["xnT_ready"], 2 * KT * b + h - 2)
                    for q in range(ST // 2):
                        i = nc.tensor.transpose(C[:, h % 3, q * P:(q + 1) * P],
                                                xe[:, n * ST // 2 + q, k * P:(k + 1) * P], ident)
                    i.then_inc(sem["tr_done"], 1)

            def rows_dt(b, k):
                pe.wait_ge(sem["xnT_ready"], 2 * KT * b + 2 * k + 2)
                for j in range(4):
                    i = nc.tensor.matmul(C[j * D:(j + 1) * D, 3, 0:S // 4], dtw[:, k, :],
                                         hs[:, k, j * S // 4:(j + 1) * S // 4], start=k == 0, stop=k == KT - 1)
                if k == KT - 1:
                    i.then_inc(sem["dt_done"], 1)

            for k in range(KT):
                transpose_x(0, k)
                if k:
                    rows_dt(0, k - 1)
            rows_dt(0, KT - 1)
            for b in range(B):
                pe.wait_ge(sem["decay_ready"], 4 * (b + 1))
                if b:
                    pe.wait_ge(sem["zve_ready"], b)
                for k in range(KT + 1):
                    if k < KT:
                        if k >= 2:
                            pe.wait_ge(sem["scanned"], KT * b + k - 1)
                        for n in range(2):
                            i = nc.tensor.matmul(pair(A, k)[:, n, :], spread_s[:, k, :], decay[:, n * HALF:(n + 1) * HALF],
                                                 start=True, stop=True)
                        i.then_inc(sem["bc_done"], 1)
                    if k:
                        pe.wait_ge(sem["scanned"], KT * b + k)
                        if k >= 3:
                            pe.wait_ge(sem["radd_done"], KT * b + k - 2)
                        dst = flat(pair(C, k - 1))
                        for st in range(ST):
                            i = nc.tensor.transpose(dst[:, st * P:(st + 1) * P], hs[:, k - 1, st * P:(st + 1) * P], ident)
                        i.then_inc(sem["back_done"], 1)
                for n in range(2):
                    pe.wait_ge(sem["norm_ready"], 2 * ST * b + ST + (n + 1) * ST // 2)
                    for k in range(KT):
                        i = n * KT + k
                        if i >= 4:
                            pe.wait_ge(sem["fn_parts"], 2 * KT * b + i - 3)
                        for q in range(ST // 2):
                            ins = nc.tensor.transpose(A[:, i % 4, q * P:(q + 1) * P],
                                                      xn[:, n * ST // 2 + q, k * P:(k + 1) * P], ident)
                            if i == 0 and q == 0:
                                ins.then_inc(sem["tileC"], 1)
                        ins.then_inc(sem["fn_tr_done"], 1)
                pe.wait_ge(sem["fn_parts"], 2 * KT * (b + 1))
                pe.wait_ge(sem["radd_done"], KT * (b + 1))

                def ff_round(g):
                    for j in range(JB):
                        pe.wait_ge(sem["w_ready"], SLABS * b + slab_pos(g, j) + 1)
                        for n in range(2):
                            i = 2 * j + n
                            if not isinstance(g, int) or g or i >= 4:
                                pe.wait_ge(sem["gelu_parts"], TILES_FF * b + 8 * g + i - 3)
                            if isinstance(g, int) and g == 0 and j == 0:
                                pe.wait_ge(sem["fn_split"], 2 * KT * b + KT * (n + 1))
                            slab_tile(i % 4, j % 2, n)
                    for st in range(ST):
                        v = ST * ROUNDS * b + ST * g + st
                        if not isinstance(v, int) or v >= 2:
                            pe.wait_ge(sem["yadded"], v - 1)
                        for j in range(JB):
                            if st == 0:
                                pe.wait_ge(sem["w_ready"], SLABS * b + 8 * g + W2_POS[j] + 1)
                                pe.wait_ge(sem["hid_split"], TILES_FF * b + 8 * g + 2 * j + 2)
                            s = slice(st * P, (st + 1) * P)
                            for n in range(2):
                                r = slice(n * HALF, (n + 1) * HALF)
                                ins = three(pair(C, st)[:, n, :], hid_hi[:, j, s], hid_lo[:, j, s], w2_hi[:, j, r],
                                            w2_lo[:, j, r], j == 0, j == JB - 1)
                        ins.then_inc(sem["tileC"], 1)

                ff_round(0)
                with pe.Fori(1, ROUNDS) as g:
                    ff_round(g)

                def gp_tiles(o):
                    for w in range(2):
                        pe.wait_ge(sem["w_ready"], SLABS * b + 2 * W1_SLABS + 2 * o + w + 1)
                        if isinstance(o, int):
                            pe.wait_ge(sem["gelu_parts"], TILES_FF * (b + 1))
                        elif w == 0:
                            pe.wait_ge(sem["g_ready"], 2 * OT * b + 2 * o)
                        else:
                            pe.wait_ge(sem["p_used"], OT * b + o)
                        for n in range(2):
                            for k in range(KT):
                                if isinstance(o, int) and w == 0 and n == 0:
                                    pe.wait_ge(sem["x1_split"], ST * b + k + 1)
                                c = slice(k * P, (k + 1) * P)
                                r = slice(n * HALF, (n + 1) * HALF)
                                ins = three(A[:, 2 * w + n, :], w1_hi[:, w, c], w1_lo[:, w, c], act_hi[:, k, r],
                                            act_lo[:, k, r], k == 0, k == KT - 1)
                            ins.then_inc(sem["tileA"], 1)

                gp_tiles(0)
                with pe.Fori(1, OT) as o:
                    gp_tiles(o)

                def t_tile(o, i):
                    if i % 2 == 0:
                        pe.wait_ge(sem["w_ready"], SLABS * b + 2 * W1_SLABS + 2 * OT + o + 1)
                    slab_tile(i % 4, (i // 2) % 2, i % 2)

                pe.wait_ge(sem["g_ready"], 2 * OT * (b + 1))
                for i in range(2):
                    t_tile(0, i)
                pe.wait_ge(sem["s3_ready"], b + 1)
                nc.tensor.matmul(C[:, 0, 0:3], ones[:], s3[:, 0:3], start=True, stop=True).then_inc(sem["tot_done"], 1)
                pe.wait_ge(sem["p_used"], OT * (b + 1))
                for i in range(2, 2 * OT):
                    if i >= 4:
                        pe.wait_ge(sem["t_used"], 2 * OT * b + i - 3)
                    t_tile(i // 2, i)
                pe.wait_ge(sem["t_used"], 2 * OT * (b + 1))
                for i in range(2 * ST):
                    q, sub, n = i // 4, (i // 2) % 2, i % 2
                    if i % 4 == 0:
                        pe.wait_ge(sem["w_ready"], SLABS * b + 2 * W1_SLABS + 3 * OT + q + 1)
                    if i >= 4:
                        pe.wait_ge(sem["z_ready"], 2 * ST * b + i - 3)
                    for k in range(OT):
                        if i < 2:
                            pe.wait_ge(sem["y_split"], 2 * OT * b + 2 * k + n + 1)
                        c = slice(k * 2 * P + sub * P, k * 2 * P + (sub + 1) * P)
                        r = slice(n * HALF, (n + 1) * HALF)
                        ins = three(A[:, i % 4, :], w1_hi[:, q % 2, c], w1_lo[:, q % 2, c], hid_hi[:, k, r],
                                    hid_lo[:, k, r], k == 0, k == OT - 1)
                    ins.then_inc(sem["tileA"], 1)
                    if b + 1 < B and i >= TR_AT:
                        transpose_x(b + 1, i - TR_AT)
                        if i > TR_AT:
                            rows_dt(b + 1, i - TR_AT - 1)
                if b + 1 < B:
                    for k in range(2 * ST - TR_AT, KT):
                        transpose_x(b + 1, k)
                        rows_dt(b + 1, k - 1)
                    rows_dt(b + 1, KT - 1)
                pe.wait_ge(sem["zmv_ready"], b + 1)
                nc.tensor.matmul(A[:, 3, 0:2], ones[:], zmv[:, 0:2], start=True, stop=True).then_inc(sem["mu_done"], 1)
                pe.wait_ge(sem["zw_ready"], b + 1)
                nc.tensor.matmul(A[:, 3, 8:9], ones[:], zw[:, 0:1], start=True, stop=True).then_inc(sem["var_done"], 1)


def kernel(**inputs):
    import numpy as np
    import concourse.bacc as bacc
    from concourse.bass_utils import run_bass_kernel_spmd

    v = {k: np.asarray(a) for k, a in inputs.items()}

    def slab(wt, width):
        r, c = wt.shape
        return wt.reshape(r // P, P, c // width, width).transpose(2, 1, 0, 3).reshape(c // width, P, r // P * width)

    wt, wp, wg, wz = (v["L1_conv_" + n].T for n in ("Wt", "Wp", "Wg", "Wz"))
    gp = np.stack([slab(wg, P), slab(wp, P)], axis=1).reshape(2 * OT, P, ED)
    by_tile = lambda a: a.reshape(-1, P).T
    eye = np.eye(P, dtype=np.float32)
    row_of = (np.arange(ED) // D)
    onehot = (row_of[:, None] == np.arange(D)[None, :]).astype(np.float32)
    arrays = {
        "x": v["x"].reshape(B, S, ED),
        "slabs": np.concatenate([slab(v["L0_conv_W1"], P), gp, slab(wt, P), slab(wz, 2 * P)], axis=0),
        "w2": v["L0_conv_W2"].reshape(W1_SLABS, P, ED),
        "cols": np.concatenate([by_tile(v[n].reshape(-1)) for n in (
            "L0_conv_g_ssm", "L0_conv_b_ssm", "L0_conv_g_ffn", "L0_conv_b_ffn", "L0_conv_bb1",
            "L1_conv_gn_w", "L1_conv_gn_b")], axis=1),
        "bb2": v["L0_conv_bb2"].reshape(ED),
        "w_dt": v["L0_conv_w_dt"].reshape(D, 1),
        "log_a": v["L0_conv_log_A"].reshape(D, 1),
        "b_dt": v["L0_conv_b_dt"].reshape(1),
        "consts": np.concatenate([eye, onehot.reshape(KT, P, D).transpose(1, 0, 2).reshape(P, KT * D)], axis=1),
        "spread": np.concatenate([onehot.T] * RPT, axis=0),
    }
    arrays = {k: np.ascontiguousarray(a) for k, a in arrays.items()}
    nc = bacc.Bacc("TRN2", target_bir_lowering=False, num_devices=1)
    args = [nc.dram_tensor(k, a.shape, mybir.dt.from_np(a.dtype), kind="ExternalInput").ap() for k, a in arrays.items()]
    out = nc.dram_tensor("out", (B, S, ED), F32, kind="ExternalOutput").ap()
    build(nc, *args, out)
    r = run_bass_kernel_spmd(nc, [arrays], core_ids=[0])
    return r.results[0]["out"].reshape(B, S, D, D)
```

```python
import math

import concourse.bass as bass
from concourse import mybir

F32 = mybir.dt.float32
F32R = mybir.dt.float32r
ACT = mybir.ActivationFunctionType
ALU = mybir.AluOpType
AX_X = mybir.AxisListType.X

P = 128
HALF = 512
B, S, ED, HID, CP = 2, 1024, 1024, 4096, 512
D = 32
ST, KT = S // P, ED // P
JB = 4
ROUNDS = HID // P // JB
OT = CP // P
RPT = P // D
LN_EPS = 1e-5
GAMMA = 1e-4
ALPHA2 = [(2.0 * GAMMA) ** k / math.factorial(k) * math.exp(-2.0 * GAMMA) for k in range(3)]

W1_SLABS = HID // P
SLABS = 2 * W1_SLABS + 4 * OT
TILES_FF = 2 * W1_SLABS
TILES_GP = TILES_FF + 4 * OT
TILES_T = TILES_GP + 2 * OT
TILES = TILES_T + 2 * ST
ROWS_Y = 1 + ST * ROUNDS
TR_AT = 1
BC_AT = 11
BACK_AT = BC_AT + KT // 2
BACKS = 2 * (2 * ST - BACK_AT)
POOL_ADDS = (1, 3, 5)
CONST_DMAS = 1 + 2 * RPT
ACT_NORM = ST // 2
NORMS = 2 * ST - ACT_NORM
X_ACT = ST // 2
C_GS, C_BS, C_GF, C_BF, C_B1, C_GN, C_BN = 0, 8, 16, 24, 32, 64, 72
COLS = 80


def build(nc, x, slabs, w2, cols, bb2, w_dt, log_a, b_dt, consts, spread, out):
    K = 1024
    start = -(-nc.sbuf_base // 64) * 64

    def at(name, offset, shape, dt=F32):
        return nc.alloc_sbuf_tensor_at(name, shape, dt, offset=start + offset)

    acc = [at("acc0", 0, [P, ST, ED]), at("acc1", 32 * K, [P, ST, ED])]
    act_hi = [at("act_hi0", 32 * K, [P, KT, S], F32R), at("act_hi1", 0, [P, KT, S], F32R)]
    act_lo = at("act_lo", 64 * K, [P, KT, S], F32R)
    xe = at("xe", 32 * K, [P, ST, ED])
    hs = at("hs", 64 * K, [P, KT, S])
    hid_hi = at("hid_hi", 96 * K, [P, JB, S], F32R)
    hid_lo = at("hid_lo", 112 * K, [P, JB, S], F32R)
    xn = at("xn", 96 * K, [P, ST, ED])
    back = at("back", 96 * K, [P, KT, S])
    gsb = at("gsb", 96 * K, [P, OT, S])
    pg = at("pg", 112 * K, [P, 2, S])
    ppg = at("ppg", 120 * K, [P, S])
    w2_hi = at("w2_hi", 128 * K, [P, JB, ED], F32R)
    w2_lo = at("w2_lo", 144 * K, [P, JB, ED], F32R)
    zsb = at("zsb", 128 * K, [P, ST, ED])
    x_land = [xe, at("x_land1", 128 * K, [P, ST, ED])]
    w1_hi = at("w1_hi", 160 * K, [P, 2, ED], F32R)
    w1_lo = at("w1_lo", 168 * K, [P, 2, ED], F32R)
    raw = at("raw", 176 * K, [P, 2, ED])
    part = at("part", 184 * K, [P, 4, HALF])
    dec = at("dec", 184 * K, [P, 2, S // 4])
    decay_hi = at("decay_hi", 186 * K, [P, S], F32R)
    decay_lo = at("decay_lo", 192 * K, [P, S], F32R)
    bb2_b = at("bb2_b", 192 * K, [P, ED])
    spread_in = at("spread_in", 128 * K, [P, KT, P])
    spread_s = at("spread_s", 196 * K, [P, KT, P], F32R)
    o = 200 * K
    const_s = at("const_s", o, [P, P + KT * D]); o += 4 * (P + KT * D)
    ones = at("ones", o, [P, P]); o += 4 * P
    dtw = at("dtw", o, [P, KT, D]); o += 4 * KT * D
    col = at("col", o, [P, COLS]); o += 4 * COLS
    wcol = at("wcol", o, [P, 8]); o += 32
    drow = at("drow", o, [P, 8]); o += 32
    st6 = at("st6", o, [P, ST, 2, 6]); o += 48 * ST
    zst = at("zst", o, [P, 2 * ST, 6]); o += 24 * 2 * ST
    mv = at("mv", o, [P, ST, 2]); o += 8 * ST
    ve = at("ve", o, [P, ST]); o += 4 * ST
    rstd = at("rstd", o, [P, ST]); o += 4 * ST
    nmr = at("nmr", o, [P, ST]); o += 4 * ST
    mhalf = at("mhalf", o, [P, 8]); o += 32
    b1g = at("b1g", o, [P, 8]); o += 32
    gsum = at("gsum", o, [P, 2 * OT]); o += 8 * OT
    psum1 = at("psum1", o, [P, 2, OT]); o += 8 * OT
    s3 = at("s3", o, [P, 8]); o += 32
    alpha2 = at("alpha2", o, [P, 8]); o += 32
    coef = at("coef", o, [P, 8]); o += 32
    zmv = at("zmv", o, [P, 8]); o += 32
    zw = at("zw", o, [P, 8]); o += 32
    zscale = at("zscale", o, [P, ST]); o += 4 * ST
    zbias = at("zbias", o, [P, ST]); o += 4 * ST
    assert start + o <= nc.sbuf_usable_end
    ident = const_s[:, 0:P]
    mask = const_s[:, P:P + KT * D].rearrange("p (k r) -> p k r", k=KT)

    A = nc.alloc_psum_tensor("A", [P, 4, HALF], F32)
    C = nc.alloc_psum_tensor("C", [P, 4, HALF], F32)

    def pair(t, i):
        return t[:, 2 * (i % 2):2 * (i % 2) + 2, :]

    def flat(ap):
        return ap.rearrange("p a c -> p (a c)")

    sem = {}
    for n in (
            "const_in", "tables_in", "spread_in", "slab_in0", "slab_in1", "xr_in", "bb2_in", "out_done",
            "ones_ready", "drow_ready", "negA_ready", "dtw_ready", "spread_ready", "alpha_ready",
            "rows_ready", "stats", "ve_ready", "rstd_ready", "nmr_ready", "norm_ready", "x_norm_act",
            "norm_act",
            "tr_done", "xnT_ready", "xnT_dve", "dt_done", "relu_ready", "abs_ready", "exp_ready", "log_ready",
            "sp_ready", "decay_zero", "decay_hi_ready", "decay_ready", "bc_done", "scanned", "back_done",
            "back_copied", "radd_done", "radd_pool",
            "fn_tr_done", "fn_parts", "fn_hi", "fn_lo", "fn_split",
            "w_hi_ready", "w_ready", "tileA", "b1_ready", "gelu_parts", "hid_split", "tileC", "yadded",
            "bb2_added",
            "x1_hi", "x1_split", "g_ready", "pg_ready", "p_used", "s3_ready", "tot_done", "coef_ready", "t_lin",
            "t_used", "y_parts", "y_split",
            "z_ready", "z_stats", "zmv_ready", "mu_done", "zw_ready", "var_done", "zve_ready", "zrstd_ready",
            "zscale_ready", "zbias_ready", "zn_ready", "add_dve", "add_pool", "dve_c"):
        sem[n] = nc.alloc_semaphore(n)
    x_in = [nc.alloc_semaphore(f"x_in{i}") for i in range(ST)]
    slab_in = [sem["slab_in0"], sem["slab_in1"]]

    def slab_pos(g, j):
        return 8 * g + (0, 1, 4, 6)[j]

    W2_POS = (2, 3, 5, 7)

    def load_slab(sp, b, pos, slot, src):
        if not (isinstance(pos, int) and pos + SLABS * b < 2):
            sp.wait_ge(sem["w_ready"], pos + SLABS * b - 1)
        sp.dma_start(raw[:, slot, :], src).then_inc(slab_in[slot], 16)

    with nc.Block() as block:
        def adds(b):
            on_pool = [1, 3, 5, 6, 7] if b + 1 < B else [1, 3, 5]
            return on_pool, [c for c in range(ST) if c not in on_pool]

        def adds_before(b, who):
            return sum(len(adds(i)[who]) for i in range(b))

        def added(b, c):
            who = 0 if c in adds(b)[0] else 1
            return ("add_pool", "add_dve")[who], adds_before(b, who) + adds(b)[who].index(c) + 1

        def xnT(b, h):
            if b:
                return "xnT_ready", 2 * KT * b - KT // 2 + h + 1
            if h < KT:
                return "xnT_ready", h + 1
            return ("xnT_dve", (h - KT) // 2 + 1) if h % 2 else ("xnT_ready", KT + (h - KT) // 2 + 1)

        def back_taken(b, k):
            if b == 0 and k in POOL_ADDS:
                return "back_copied", POOL_ADDS.index(k) + 1
            return "radd_done", KT * b + k + 1 - sum(b > 0 or p < k for p in POOL_ADDS)

        @block.sync
        def _(sp):
            def load_x(b, dst, sems, tiles=range(ST)):
                for st in tiles:
                    sp.dma_start(dst[:, st, :], x[b, st * P:(st + 1) * P, :]).then_inc(sems[st % len(sems)], 16)

            for dst, src in ((const_s[:], consts), (col[:], cols)):
                sp.dma_start(dst, src).then_inc(sem["tables_in"], 16)
            load_x(0, x_land[0], x_in)
            sp.dma_start(spread_in[:].rearrange("r k p -> r (k p)"), spread).then_inc(sem["spread_in"], 16)
            load_slab(sp, 0, 0, 0, slabs[0])
            load_slab(sp, 0, 1, 1, slabs[1])
            load_x(0, acc[0], [sem["xr_in"]])
            def load_bb2(b):
                sp.wait_ge(sem["bc_done"], KT * (b + 1))
                sp.dma_start(bb2_b[:], bb2.partition_broadcast(P)).then_inc(sem["bb2_in"], 16)

            load_bb2(0)
            for b in range(B):
                with sp.Fori(0, ROUNDS) as g:
                    p0 = 8 * g + 2
                    load_slab(sp, b, p0, 0, w2[JB * g])
                    load_slab(sp, b, p0 + 1, 1, w2[JB * g + 1])
                    load_slab(sp, b, p0 + 2, 0, slabs[JB * g + 2])
                    load_slab(sp, b, p0 + 3, 1, w2[JB * g + 2])
                    load_slab(sp, b, p0 + 4, 0, slabs[JB * g + 3])
                    load_slab(sp, b, p0 + 5, 1, w2[JB * g + 3])
                    load_slab(sp, b, p0 + 6, 0, slabs[JB * g + 4])
                    load_slab(sp, b, p0 + 7, 1, slabs[JB * g + 5])
                for m in range(W1_SLABS + 2, W1_SLABS + 4 * OT):
                    load_slab(sp, b, m + W1_SLABS, m % 2, slabs[m])
                    x0 = 2 * (m - W1_SLABS - 3)
                    if b + 1 < B and 0 <= x0 < ST:
                        if x0 == 0:
                            sp.wait_ge(sem["tileC"], ROWS_Y * (b + 1))
                        load_x(b + 1, x_land[b + 1], x_in, range(x0, x0 + 2))
                if b + 1 < B:
                    load_slab(sp, b + 1, 0, 0, slabs[0])
                    load_slab(sp, b + 1, 1, 1, slabs[1])
                    sp.wait_ge(sem["tr_done"], 2 * KT * (b + 2))
                    load_x(b + 1, acc[b + 1], [sem["xr_in"]])
                    load_bb2(b + 1)
                for c in range(ST):
                    name, v = added(b, c)
                    sp.wait_ge(sem[name], v)
                    sp.dma_start(out[b, c * P:(c + 1) * P, :], zsb[:, c, :]).then_inc(sem["out_done"], 16)
            sp.wait_ge(sem["out_done"], 16 * ST * B)

        def fn_cut(i):
            return (slice(None), i % KT, slice(i // KT * HALF, (i // KT + 1) * HALF))

        def fn_bank(i):
            if i < KT:
                return C[:, i % 4, :]
            i = (i - KT) % 6
            return A[:, 2 * i + 1, :] if i < 2 else C[:, i - 2, :]

        @block.gpsimd
        def _(pool):
            pool.memset(ones[:], 1.0).then_inc(sem["ones_ready"], 1)
            pool.memset(mhalf[:], -0.5).then_inc(sem["ones_ready"], 1)

            def low(b, pos, slot, hi, lo):
                pool.wait_ge(sem["w_hi_ready"], SLABS * b + pos + 1)
                nc.gpsimd.tensor_tensor(lo, raw[:, slot, :], hi.bitcast(F32), ALU.subtract).then_inc(sem["w_ready"], 1)

            def low1(b, pos, ring):
                low(b, pos, pos % 2, w1_hi[:, ring, :], w1_lo[:, ring, :])

            def inv_std(n, tiles, negative_mean=False, together=1):
                for st in tiles[::together]:
                    c = slice(st, st + together)
                    pool.wait_ge(sem["stats"], n + st + together)
                    nc.gpsimd.tensor_scalar(ve[:, c], mv[:, c, 1], LN_EPS, None, ALU.add).then_inc(sem["ve_ready"], together)
                    pool.wait_ge(sem["ve_ready"], n + st + together)
                    nc.gpsimd.tensor_tensor(rstd[:, c], ve[:, c], mhalf[:, 0:together], ALU.pow)\
                        .then_inc(sem["rstd_ready"], together)
                    if negative_mean and st < ACT_NORM:
                        pool.wait_ge(sem["rstd_ready"], n + st + together)
                        for t in range(st, st + together):
                            nc.gpsimd.tensor_scalar(nmr[:, t:t + 1], mv[:, t, 0:1], rstd[:, t:t + 1], -1.0, ALU.mult, ALU.mult)\
                                .then_inc(sem["nmr_ready"], 1)

            def z_inv_std(b):
                pool.wait_ge(sem["zve_ready"], b + 1)
                nc.gpsimd.tensor_tensor(zw[:, 3:4], zw[:, 2:3], mhalf[:, 0:1], ALU.pow).then_inc(sem["zrstd_ready"], 1)

            def z_adds(b, tiles):
                for c in tiles:
                    pool.wait_ge(sem["zn_ready"], ST * b + c + 1)
                    nc.gpsimd.tensor_tensor(zsb[:, c, :], zsb[:, c, :], acc[b][:, c, :], ALU.add)\
                        .then_inc(sem["add_pool"], 1)

            def clear_decay():
                for part_of in (decay_hi, decay_lo):
                    nc.gpsimd.memset(part_of[:].bitcast(F32), 0.0).then_inc(sem["decay_zero"], 1)

            clear_decay()
            pool.wait_ge(sem["ones_ready"], 2)
            inv_std(0, range(ST), negative_mean=True)
            low1(0, 0, 0)
            low1(0, 1, 1)
            for b in range(B):
                n0 = 2 * ST * b + ST
                if b == 0:
                    pool.wait_ge(sem["xr_in"], 16 * ST)
                    for i, k in enumerate(POOL_ADDS):
                        c = slice(k * P, (k + 1) * P)
                        pool.wait_ge(sem["back_copied"], i + 1)
                        nc.gpsimd.tensor_tensor(acc[0][:, :, c], back[:, k, :].rearrange("p (s c) -> p s c", s=ST),
                                                acc[0][:, :, c], ALU.add).then_inc(sem["radd_pool"], 1)
                    inv_std(n0, range(ST), negative_mean=True)
                else:
                    on_pool = adds(b - 1)[0]
                    z_inv_std(b - 1)
                    z_adds(b - 1, on_pool[:2])
                    inv_std(n0, range(ST // 2), negative_mean=True, together=2)
                    z_adds(b - 1, on_pool[2:3])
                    inv_std(n0, range(ST // 2, ST), together=4)
                    z_adds(b - 1, on_pool[3:])
                for i in range(1, 2 * KT, 2):
                    cut = fn_cut(i)
                    pool.wait_ge(sem["fn_hi"], 2 * KT * b + i + 1)
                    nc.gpsimd.tensor_tensor(act_lo[cut], part[:, i % 4, :], act_hi[b][cut].bitcast(F32), ALU.subtract)\
                        .then_inc(sem["fn_lo"], 1)
                with pool.Fori(0, ROUNDS) as g:
                    low(b, 8 * g + 2, 0, w2_hi[:, 0, :], w2_lo[:, 0, :])
                    low(b, 8 * g + 3, 1, w2_hi[:, 1, :], w2_lo[:, 1, :])
                    low(b, 8 * g + 4, 0, w1_hi[:, 0, :], w1_lo[:, 0, :])
                    low(b, 8 * g + 5, 1, w2_hi[:, 2, :], w2_lo[:, 2, :])
                    low(b, 8 * g + 6, 0, w1_hi[:, 1, :], w1_lo[:, 1, :])
                    low(b, 8 * g + 7, 1, w2_hi[:, 3, :], w2_lo[:, 3, :])
                    low(b, 8 * g + 8, 0, w1_hi[:, 0, :], w1_lo[:, 0, :])
                    low(b, 8 * g + 9, 1, w1_hi[:, 1, :], w1_lo[:, 1, :])
                for m in range(W1_SLABS + 2, W1_SLABS + 4 * OT):
                    if b + 1 < B and W1_SLABS + 3 * OT <= m < W1_SLABS + 3 * OT + 2:
                        h = (m - W1_SLABS - 3 * OT) * ST // 2
                        inv_std(2 * ST * (b + 1), range(h, h + ST // 2))
                    if b + 1 < B and m == W1_SLABS + 4 * OT - 2:
                        pool.wait_ge(sem["y_split"], 2 * OT * (b + 1))
                        clear_decay()
                    low1(b, m + W1_SLABS, m % 2)
                if b + 1 < B:
                    low1(b + 1, 0, 0)
                    low1(b + 1, 1, 1)
            z_inv_std(B - 1)
            z_adds(B - 1, adds(B - 1)[0])

        @block.scalar
        def _(act):
            def high(b, pos, loads, slot, dst, free):
                act.wait_ge(slab_in[slot], 16 * loads)
                if free:
                    act.wait_ge(sem[free[0]], free[1])
                nc.scalar.activation(dst, raw[:, slot, :], ACT.Copy).then_inc(sem["w_hi_ready"], 1)

            def high1(b, m):
                pos = m if m < 2 else m + W1_SLABS
                last = m - 2 if m >= 2 else m + W1_SLABS + 4 * OT - 2
                done = 2 * (last + 1) if last < W1_SLABS + 3 * OT else TILES_T + 4 * (last - W1_SLABS - 3 * OT + 1)
                done += TILES * (b if m >= 2 else b - 1)
                high(b, pos, SLABS // 2 * b + pos // 2 + 1, pos % 2, w1_hi[:, m % 2, :], ("tileA", done) if done > 0 else None)

            def transposed(b, h):
                k, n = h % KT, h // KT
                act.wait_ge(sem["tr_done"], 2 * KT * b + h + 1)
                nc.scalar.activation(hs[:, k, n * HALF:(n + 1) * HALF], C[:, h % 3, :], ACT.Identity,
                                     bias=col[:, C_BS + k:C_BS + k + 1], scale=col[:, C_GS + k:C_GS + k + 1])\
                    .then_inc(sem["xnT_ready"], 1)

            def z_norm(b):
                act.wait_ge(sem["zbias_ready"], b + 1)
                for c in range(ST):
                    nc.scalar.activation(zsb[:, c, :], zsb[:, c, :], ACT.Identity, bias=zbias[:, c:c + 1],
                                         scale=zscale[:, c:c + 1]).then_inc(sem["zn_ready"], 1)

            act.dma_start(drow[:, 2:3], b_dt.partition_broadcast(P)).then_inc(sem["const_in"], 16)
            for q in range(RPT):
                act.dma_start(wcol[q * D:(q + 1) * D, 0:1], w_dt).then_inc(sem["const_in"], 16)
                act.dma_start(drow[q * D:(q + 1) * D, 0:1], log_a).then_inc(sem["const_in"], 16)
            for st in range(X_ACT):
                act.wait_ge(sem["nmr_ready"], st + 1)
                nc.scalar.activation(xe[:, st, :], xe[:, st, :], ACT.Identity, bias=nmr[:, st:st + 1],
                                     scale=rstd[:, st:st + 1]).then_inc(sem["x_norm_act"], 1)
            act.wait_ge(sem["const_in"], 16 * CONST_DMAS)
            nc.scalar.activation(drow[:, 1:2], drow[:, 0:1], ACT.Exp).then_inc(sem["drow_ready"], 1)
            act.wait_ge(sem["drow_ready"], 1)
            nc.scalar.activation(drow[:, 3:4], drow[:, 1:2], ACT.Copy, scale=-1.0).then_inc(sem["negA_ready"], 1)
            act.wait_ge(sem["negA_ready"], 1)
            act.wait_ge(sem["ones_ready"], 2)
            act.wait_ge(sem["tables_in"], 32)
            for h in range(2 * KT):
                if xnT(0, h)[0] == "xnT_ready":
                    transposed(0, h)

            def decays(b):
                act.wait_ge(sem["abs_ready"], b + 1)
                nc.scalar.activation(dec[:, 0, :], dec[:, 0, :], ACT.Exp).then_inc(sem["exp_ready"], 1)
                act.wait_ge(sem["exp_ready"], b + 1)
                nc.scalar.activation(dec[:, 0, :], dec[:, 0, :], ACT.Ln, bias=ones[:, 0:1]).then_inc(sem["log_ready"], 1)
                act.wait_ge(sem["sp_ready"], b + 1)
                nc.scalar.activation(dec[:, 0, :], dec[:, 1, :], ACT.Exp, scale=drow[:, 3:4])
                act.wait_ge(sem["decay_zero"], 2 * (b + 1))
                for j in range(4):
                    q = slice(j * D, (j + 1) * D)
                    nc.scalar.activation(decay_hi[q, j * S // 4:(j + 1) * S // 4], dec[q, 1, :], ACT.Exp, scale=drow[q, 3:4])\
                        .then_inc(sem["decay_hi_ready"], 1)

            decays(0)
            high1(0, 0)
            high1(0, 1)
            for k in POOL_ADDS:
                act.wait_ge(sem["back_done"], k + 1)
                nc.scalar.activation(back[:, k, :], flat(pair(C, k)), ACT.Copy).then_inc(sem["back_copied"], 1)
            for b in range(B):
                if b:
                    z_norm(b - 1)
                for st in range(ACT_NORM):
                    act.wait_ge(sem["nmr_ready"], X_ACT + ACT_NORM * b + st + 1)
                    nc.scalar.activation(xn[:, st, :], acc[b][:, st, :], ACT.Identity, bias=nmr[:, st:st + 1],
                                         scale=rstd[:, st:st + 1]).then_inc(sem["norm_act"], 1)
                for i in range(2 * KT):
                    k = i % KT
                    act.wait_ge(sem["fn_tr_done"], 2 * KT * b + i + 1)
                    if i >= 4:
                        act.wait_ge(sem["fn_lo" if i % 2 else "fn_split"], KT * b + (i - 4) // 2 + 1)
                    nc.scalar.activation(part[:, i % 4, :], fn_bank(i), ACT.Identity, bias=col[:, C_BF + k:C_BF + k + 1],
                                         scale=col[:, C_GF + k:C_GF + k + 1]).then_inc(sem["fn_parts"], 1)
                if b:
                    act.wait_ge(sem["out_done"], 16 * ST * b)
                act.wait_ge(sem["fn_split"], KT * (b + 1))
                act.wait_ge(sem["fn_lo"], KT * (b + 1))

                def gelus(g, j):
                    for n in range(2):
                        i = 2 * j + n
                        u = TILES_FF * b + 8 * g + i
                        act.wait_ge(sem["tileA"], TILES * b + 8 * g + (3 if isinstance(g, int) and i == 1 else i + 1))
                        if not isinstance(u, int) or u >= 4:
                            act.wait_ge(sem["hid_split"], u - 3)
                        nc.scalar.activation(part[:, i % 4, :], A[:, i % 4, :], ACT.Gelu, bias=b1g[:, j:j + 1])
                        nc.scalar.activation(hid_hi[:, j, n * HALF:(n + 1) * HALF], A[:, i % 4, :], ACT.Gelu,
                                             bias=b1g[:, j:j + 1]).then_inc(sem["gelu_parts"], 1)

                def ff_round(g):
                    n0 = SLABS // 2 * b + 4 * g + 2
                    u0 = TILES * b + 8 * g
                    last = ("tileC", ROWS_Y * b + ST * g + 1)
                    high(b, 8 * g + 2, n0, 0, w2_hi[:, 0, :], last)
                    high(b, 8 * g + 3, n0, 1, w2_hi[:, 1, :], None)
                    act.wait_ge(sem["b1_ready"], ROUNDS * b + g + 1)
                    gelus(g, 0)
                    high(b, 8 * g + 4, n0 + 1, 0, w1_hi[:, 0, :], ("tileA", u0 + (3 if isinstance(g, int) else 2)))
                    high(b, 8 * g + 5, n0 + 1, 1, w2_hi[:, 2, :], None)
                    gelus(g, 1)
                    high(b, 8 * g + 6, n0 + 2, 0, w1_hi[:, 1, :], ("tileA", u0 + 4))
                    high(b, 8 * g + 7, n0 + 2, 1, w2_hi[:, 3, :], None)
                    gelus(g, 2)
                    gelus(g, 3)
                    high(b, 8 * g + 8, n0 + 3, 0, w1_hi[:, 0, :], ("tileA", u0 + 6))
                    high(b, 8 * g + 9, n0 + 3, 1, w1_hi[:, 1, :], ("tileA", u0 + 8))

                ff_round(0)
                with act.Fori(1, ROUNDS) as g:
                    ff_round(g)
                for st in range(ST):
                    act.wait_ge(sem["yadded"], ST * ROUNDS * (b + 1) - ST + st + 1)
                    nc.scalar.activation(act_hi[b][:, st, :], acc[b][:, st, :], ACT.Copy).then_inc(sem["x1_hi"], 1)
                act.wait_ge(sem["tileC"], ROWS_Y * (b + 1))
                for o in range(OT):
                    for n in range(2):
                        act.wait_ge(sem["tileA"], TILES * b + TILES_FF + 4 * o + n + 1)
                        nc.scalar.activation(gsb[:, o, n * HALF:(n + 1) * HALF], A[:, n, :], ACT.Copy,
                                             accum_out=gsum[:, 2 * o + n:2 * o + n + 1]).then_inc(sem["g_ready"], 1)
                    high1(b, W1_SLABS + 2 * o + 2)
                    high1(b, W1_SLABS + 2 * o + 3)
                for i in range(2 * OT):
                    act.wait_ge(sem["t_used"], 2 * OT * b + i + 1)
                    nc.scalar.activation(part[:, i % 4, :], part[:, i % 4, :], ACT.Identity, bias=coef[:, 0:1])\
                        .then_inc(sem["y_parts"], 1)
                    act.wait_ge(sem["y_parts"], 2 * (2 * OT * b + i) + 1)
                    nc.scalar.activation(hid_hi[:, i // 2, (i % 2) * HALF:(i % 2 + 1) * HALF], part[:, i % 4, :],
                                         ACT.Copy).then_inc(sem["y_parts"], 1)
                    if i % 2:
                        high1(b, W1_SLABS + 2 * OT + 2 + i // 2)
                for i in range(2 * ST):
                    act.wait_ge(sem["tileA"], TILES * b + TILES_T + i + 1)
                    if b + 1 < B and i % 2 == 0:
                        act.wait_ge(sem["norm_ready"], NORMS * (b + 1) - X_ACT + i // 2 + 1)
                    nc.scalar.activation(zsb[:, i // 2, (i % 2) * HALF:(i % 2 + 1) * HALF], A[:, i % 4, :], ACT.Copy)\
                        .then_inc(sem["z_ready"], 1)
                    if b + 1 < B and TR_AT <= i < TR_AT + KT:
                        transposed(b + 1, 2 * (i - TR_AT))
                        transposed(b + 1, 2 * (i - TR_AT) + 1)
                    if b + 1 < B and i == TR_AT + KT - 1:
                        decays(b + 1)
                    if i % 4 == 3 and i < 8:
                        high1(b, W1_SLABS + 3 * OT + 2 + i // 4)
                    elif i == 11 and b + 1 < B:
                        high1(b + 1, 0)
                if b + 1 < B:
                    high1(b + 1, 1)
            z_norm(B - 1)

        @block.vector
        def _(dve):
            chain = [0]

            def link(ins):
                chain[0] += 1
                ins.then_inc(sem["dve_c"], 1)
                dve.wait_ge(sem["dve_c"], chain[0])

            for k in range(3):
                nc.vector.memset(alpha2[:, k:k + 1], ALPHA2[k]).then_inc(sem["alpha_ready"], 1)
            dve.wait_ge(sem["alpha_ready"], 3)

            def normalise(n, st, src, dst):
                dve.wait_ge(sem["rstd_ready"], n + st + 1)
                nc.vector.tensor_scalar(dst[:, st, :], src[:, st, :], mv[:, st, 0:1], rstd[:, st:st + 1],
                                        ALU.subtract, ALU.mult).then_inc(sem["norm_ready"], 1)

            def split_part(i, name, v, dst):
                dve.wait_ge(sem[name], v)
                return nc.vector.tensor_tensor(dst[0], part[:, i % 4, :], dst[1].bitcast(F32), ALU.subtract)

            def minus_abs(b):
                dve.wait_ge(sem["dt_done"], b + 1)
                V = C[:, 3, 0:S // 4]
                nc.vector.tensor_scalar(dec[:, 0, :], V, drow[:, 2:3], 0.0, ALU.add, ALU.min)
                nc.vector.tensor_scalar(dec[:, 1, :], V, drow[:, 2:3], 0.0, ALU.add, ALU.max).then_inc(sem["relu_ready"], 1)
                dve.wait_ge(sem["relu_ready"], b + 1)
                nc.vector.tensor_tensor(dec[:, 0, :], dec[:, 0, :], dec[:, 1, :], ALU.subtract).then_inc(sem["abs_ready"], 1)

            def tile_stats(n, st, src):
                for h in range(2):
                    i = nc.vector.bn_stats(st6[:, st, h, :], src[:, st, h * HALF:(h + 1) * HALF])
                i.then_inc(sem["rows_ready"], 1)

            def tile_mv(n, st):
                dve.wait_ge(sem["rows_ready"], n + st + 1)
                nc.vector.bn_aggr(mv[:, st, :], st6[:, st, :, :].rearrange("p a c -> p (a c)")).then_inc(sem["stats"], 1)

            def x_stats(b, st):
                dve.wait_ge(x_in[st], 16 * (b + 1))
                tile_stats(2 * ST * b, st, x_land[b])
                if st:
                    tile_mv(2 * ST * b, st - 1)

            def z_add(b, c):
                dve.wait_ge(sem["zn_ready"], ST * b + c + 1)
                nc.vector.tensor_tensor(zsb[:, c, :], zsb[:, c, :], acc[b][:, c, :], ALU.add).then_inc(sem["add_dve"], 1)

            for st in range(ST):
                x_stats(0, st)
                if st - 2 >= X_ACT:
                    normalise(0, st - 2, xe, xe)
                if st == ST - 2:
                    dve.wait_ge(sem["tables_in"], 32)
                    dve.wait_ge(sem["const_in"], 16 * CONST_DMAS)
                    nc.vector.tensor_scalar(dtw[:], mask, wcol[:, 0:1], None, ALU.mult).then_inc(sem["dtw_ready"], 1)
            tile_mv(0, ST - 1)
            for st in range(ST - 2, ST):
                normalise(0, st, xe, xe)
            for h in range(2 * KT):
                if xnT(0, h)[0] == "xnT_dve":
                    k = h % KT
                    dve.wait_ge(sem["tr_done"], h + 1)
                    nc.vector.tensor_scalar(hs[:, k, HALF:2 * HALF], C[:, h % 3, :], col[:, C_GS + k:C_GS + k + 1],
                                            col[:, C_BS + k:C_BS + k + 1], ALU.mult, ALU.add).then_inc(sem["xnT_dve"], 1)
            minus_abs(0)
            def softplus(b):
                dve.wait_ge(sem["log_ready"], b + 1)
                nc.vector.tensor_tensor(dec[:, 1, :], dec[:, 1, :], dec[:, 0, :], ALU.add).then_inc(sem["sp_ready"], 1)

            def decay_split(b):
                dve.wait_ge(sem["decay_zero"], 2 * (b + 1))
                for j in range(4):
                    cut = (slice(j * D, (j + 1) * D), slice(j * S // 4, (j + 1) * S // 4))
                    dve.wait_ge(sem["decay_hi_ready"], 4 * b + j + 1)
                    nc.vector.tensor_tensor(decay_lo[cut], dec[cut[0], 0, :], decay_hi[cut].bitcast(F32), ALU.subtract)\
                        .then_inc(sem["decay_ready"], 1)

            softplus(0)
            dve.wait_ge(sem["spread_in"], 16)
            nc.vector.tensor_copy(spread_s[:], spread_in[:]).then_inc(sem["spread_ready"], 1)
            decay_split(0)

            def scan(b, k):
                dve.wait_ge(sem["bc_done"], KT * b + k + 1)
                nc.vector.tensor_tensor_scan(hs[:, k, :], flat(pair(C if b else A, k)), hs[:, k, :], 0.0, ALU.mult, ALU.add)\
                    .then_inc(sem["scanned"], 1)

            def residual(b, k):
                dve.wait_ge(sem["xr_in"], 16 * ST * (b + 1))
                dve.wait_ge(sem["back_done"], KT * b + k + 1)
                c = slice(k * P, (k + 1) * P)
                nc.vector.tensor_tensor(acc[b][:, :, c], flat(pair(C, k)).rearrange("p (s c) -> p s c", s=ST),
                                        acc[b][:, :, c], ALU.add).then_inc(sem["radd_done"], 1)

            for b in range(B):
                n0 = 2 * ST * b
                if b == 0:
                    for k in range(KT + 1):
                        if k < KT:
                            scan(0, k)
                        if k and k - 1 not in POOL_ADDS:
                            residual(0, k - 1)
                    dve.wait_ge(sem["radd_pool"], len(POOL_ADDS))
                else:
                    for k in range(BACKS + 2, KT):
                        residual(b, k)
                dve.wait_ge(sem["radd_done"], back_taken(b, KT - 1)[1])

                def ln_stats(st):
                    tile_stats(n0 + ST, st, acc[b])
                    if st:
                        tile_mv(n0 + ST, st - 1)

                def fn_part(i):
                    if i < 2 * KT:
                        if b and i < KT:
                            name, v = added(b - 1, i)
                            dve.wait_ge(sem[name], v)
                        dve.wait_ge(sem["fn_parts"], 2 * KT * b + i + 1)
                        nc.vector.tensor_copy(act_hi[b][fn_cut(i)], part[:, i % 4, :]).then_inc(sem["fn_hi"], 1)
                    if i % 2:
                        h = i - 1
                        split_part(h, "fn_hi", 2 * KT * b + h + 1, (act_lo[fn_cut(h)], act_hi[b][fn_cut(h)]))\
                            .then_inc(sem["fn_split"], 1)

                for st in range(ST):
                    ln_stats(st)
                tile_mv(n0 + ST, ST - 1)
                if b:
                    for c in adds(b - 1)[1]:
                        z_add(b - 1, c)
                for i in range(2 * KT):
                    fn_part(i)
                    if i < ST - ACT_NORM:
                        normalise(n0 + ST, ACT_NORM + i, acc[b], xn)
                dve.wait_ge(sem["norm_act"], ACT_NORM * (b + 1))

                def hid_parts(g):
                    for i in range(2 * JB):
                        cut = (slice(None), i // 2, slice((i % 2) * HALF, (i % 2 + 1) * HALF))
                        split_part(i, "gelu_parts", TILES_FF * b + 8 * g + i + 1, (hid_lo[cut], hid_hi[cut]))\
                            .then_inc(sem["hid_split"], 1)

                def round_bias(g):
                    nc.vector.tensor_scalar(b1g[:, 0:JB], col[:, bass.ds(C_B1 + JB * g, JB)], 0.0, None, ALU.add)\
                        .then_inc(sem["b1_ready"], 1)

                round_bias(0)

                def add_y(g, st):
                    dve.wait_ge(sem["tileC"], ROWS_Y * b + ST * g + st + 2)
                    nc.vector.tensor_tensor(acc[b][:, st, :], flat(pair(C, st)), acc[b][:, st, :], ALU.add)\
                        .then_inc(sem["yadded"], 1)

                def x1_part(st):
                    dve.wait_ge(sem["x1_hi"], ST * b + st + 1)
                    nc.vector.tensor_tensor(act_lo[:, st, :], acc[b][:, st, :], act_hi[b][:, st, :].bitcast(F32), ALU.subtract)\
                        .then_inc(sem["x1_split"], 1)

                with dve.Fori(0, ROUNDS - 1) as g:
                    hid_parts(g)
                    round_bias(g + 1)
                    for st in range(ST):
                        add_y(g, st)
                    dve.wait_ge(sem["yadded"], ST * ROUNDS * b + ST * g + ST)
                dve.wait_ge(sem["bb2_in"], 16 * (b + 1))
                for st in range(ST):
                    nc.vector.tensor_tensor(acc[b][:, st, :], acc[b][:, st, :], bb2_b[:], ALU.add).then_inc(sem["bb2_added"], 1)
                hid_parts(ROUNDS - 1)
                dve.wait_ge(sem["bb2_added"], ST * (b + 1))
                for st in range(ST):
                    add_y(ROUNDS - 1, st)
                    if st:
                        x1_part(st - 1)
                x1_part(ST - 1)
                for o in range(OT):
                    dve.wait_ge(sem["g_ready"], 2 * OT * b + 2 * o + 2)
                    dve.wait_ge(sem["tileA"], TILES * b + TILES_FF + 4 * o + 4)
                    pp = flat(A[:, 2:4, :])
                    nc.vector.tensor_tensor_reduce(out=pg[:, o % 2, :], in0=pp, in1=gsb[:, o, :], scale=1.0, scalar=0.0,
                                                   op0=ALU.mult, op1=ALU.add, accum_out=psum1[:, 0, o:o + 1])\
                        .then_inc(sem["pg_ready"], 1)
                    dve.wait_ge(sem["pg_ready"], OT * b + o + 1)
                    if o:
                        dve.wait_ge(sem["p_used"], OT * b + o)
                    nc.vector.tensor_tensor_reduce(out=ppg[:], in0=pp, in1=pg[:, o % 2, :], scale=1.0, scalar=0.0,
                                                   op0=ALU.mult, op1=ALU.add, accum_out=psum1[:, 1, o:o + 1])\
                        .then_inc(sem["p_used"], 1)
                dve.wait_ge(sem["p_used"], OT * (b + 1))
                link(nc.vector.reduce_sum(s3[:, 0:1], gsum[:], AX_X))
                nc.vector.reduce_sum(s3[:, 1:3], psum1[:], AX_X).then_inc(sem["s3_ready"], 1)
                dve.wait_ge(sem["tot_done"], b + 1)
                nc.vector.tensor_tensor(coef[:, 0:3], C[:, 0, 0:3], alpha2[:, 0:3], ALU.mult).then_inc(sem["coef_ready"], 1)
                dve.wait_ge(sem["coef_ready"], b + 1)
                for i in range(2 * OT + 1):
                    if i < 2 * OT:
                        dve.wait_ge(sem["tileA"], TILES * b + TILES_GP + i + 1)
                        if i >= 4:
                            dve.wait_ge(sem["y_split"], 2 * OT * b + i - 3)
                        nc.vector.tensor_scalar(part[:, i % 4, :], A[:, i % 4, :], coef[:, 2:3], coef[:, 1:2],
                                                ALU.mult, ALU.add).then_inc(sem["t_lin"], 1)
                        dve.wait_ge(sem["t_lin"], 2 * OT * b + i + 1)
                        nc.vector.tensor_tensor(part[:, i % 4, :], A[:, i % 4, :], part[:, i % 4, :], ALU.mult)\
                            .then_inc(sem["t_used"], 1)
                    if i:
                        h = i - 1
                        cut = (slice(None), h // 2, slice((h % 2) * HALF, (h % 2 + 1) * HALF))
                        split_part(h, "y_parts", 2 * (2 * OT * b + i), (hid_lo[cut], hid_hi[cut])).then_inc(sem["y_split"], 1)
                    if b + 1 < B and i < ST:
                        x_stats(b + 1, i)
                if b + 1 < B:
                    n1 = 2 * ST * (b + 1)
                    tile_mv(n1, ST - 1)
                    dve.wait_ge(sem["tileA"], TILES * b + TILES_T)
                    for st in range(ST // 2):
                        normalise(n1, st, x_land[b + 1], xe)
                for i in range(2 * ST):
                    dve.wait_ge(sem["z_ready"], 2 * ST * b + i + 1)
                    nc.vector.bn_stats(zst[:, i, :], zsb[:, i // 2, (i % 2) * HALF:(i % 2 + 1) * HALF])\
                        .then_inc(sem["z_stats"], 1)
                    if b + 1 < B:
                        if i == 0:
                            for st in range(ST // 2, ST):
                                normalise(n1, st, x_land[b + 1], xe)
                        elif i == TR_AT + KT - 1:
                            minus_abs(b + 1)
                            softplus(b + 1)
                            decay_split(b + 1)
                        elif i >= BACK_AT:
                            residual(b + 1, 2 * (i - BACK_AT))
                            residual(b + 1, 2 * (i - BACK_AT) + 1)
                        elif i >= BC_AT:
                            scan(b + 1, 2 * (i - BC_AT))
                            scan(b + 1, 2 * (i - BC_AT) + 1)
                dve.wait_ge(sem["z_stats"], 2 * ST * (b + 1))
                nc.vector.bn_aggr(zmv[:, 0:2], zst[:].rearrange("p a c -> p (a c)")).then_inc(sem["zmv_ready"], 1)
                dve.wait_ge(sem["zmv_ready"], b + 1)
                if b + 1 < B:
                    residual(b + 1, BACKS)
                dve.wait_ge(sem["mu_done"], b + 1)
                link(nc.vector.tensor_scalar(zmv[:, 2:3], A[:, 3, 0:1], 1.0 / P, None, ALU.mult))
                link(nc.vector.tensor_tensor(zmv[:, 3:4], zmv[:, 0:1], zmv[:, 2:3], ALU.subtract))
                link(nc.vector.tensor_tensor(zmv[:, 4:5], zmv[:, 3:4], zmv[:, 3:4], ALU.mult))
                nc.vector.tensor_tensor(zw[:, 0:1], zmv[:, 4:5], zmv[:, 1:2], ALU.add).then_inc(sem["zw_ready"], 1)
                if b + 1 < B:
                    residual(b + 1, BACKS + 1)
                dve.wait_ge(sem["var_done"], b + 1)
                nc.vector.tensor_scalar(zw[:, 2:3], A[:, 3, 8:9], 1.0 / P, LN_EPS, ALU.mult, ALU.add)\
                    .then_inc(sem["zve_ready"], 1)
                dve.wait_ge(sem["zrstd_ready"], b + 1)
                nc.vector.tensor_scalar(zscale[:], col[:, C_GN:C_GN + ST], zw[:, 3:4], None, ALU.mult)\
                    .then_inc(sem["zscale_ready"], 1)
                dve.wait_ge(sem["zscale_ready"], b + 1)
                link(nc.vector.tensor_scalar(zbias[:], zscale[:], zmv[:, 2:3], -1.0, ALU.mult, ALU.mult))
                nc.vector.tensor_tensor(zbias[:], zbias[:], col[:, C_BN:C_BN + ST], ALU.add).then_inc(sem["zbias_ready"], 1)
            for c in adds(B - 1)[1]:
                z_add(B - 1, c)

        @block.tensor
        def _(pe):
            def three(dst, hi, lo, rhs_hi, rhs_lo, first, last):
                nc.tensor.matmul(dst, hi, rhs_hi, start=first, stop=False)
                nc.tensor.matmul(dst, hi, rhs_lo, start=False, stop=False)
                return nc.tensor.matmul(dst, lo, rhs_hi, start=False, stop=last)

            def slab_tile(bank, ring, n, off=0, kn=KT, width=P, before=None):
                for k in range(kn):
                    if before:
                        before(n, k)
                    c = slice(k * width + off, k * width + off + P)
                    r = slice(n * HALF, (n + 1) * HALF)
                    last = three(A[:, bank, :], w1_hi[:, ring, c], w1_lo[:, ring, c], act_hi[b][:, k, r], act_lo[:, k, r],
                                 k == 0, k == kn - 1)
                return last.then_inc(sem["tileA"], 1)

            pe.wait_ge(sem["tables_in"], 32)
            pe.wait_ge(sem["ones_ready"], 2)

            def transpose_x(b, h):
                k, n = h % KT, h // KT
                if k == 0 and b == 0 and n == 0:
                    pe.wait_ge(sem["x_norm_act"], X_ACT)
                elif k == 0:
                    pe.wait_ge(sem["norm_ready"], NORMS * b - X_ACT + ST // 2 * (n + 1))
                if h >= 3:
                    name, v = xnT(b, h - 3)
                    pe.wait_ge(sem[name], v)
                for q in range(ST // 2):
                    i = nc.tensor.transpose(C[:, h % 3, q * P:(q + 1) * P],
                                            xe[:, n * ST // 2 + q, k * P:(k + 1) * P], ident)
                i.then_inc(sem["tr_done"], 1)

            def rows_dt(b, h):
                k, n = h % KT, h // KT
                name, v = xnT(b, h)
                pe.wait_ge(sem[name], v)
                for j in (2 * n, 2 * n + 1):
                    i = nc.tensor.matmul(C[j * D:(j + 1) * D, 3, 0:S // 4], dtw[:, k, :],
                                         hs[:, k, j * S // 4:(j + 1) * S // 4], start=k == 0, stop=k == KT - 1)
                if h == 2 * KT - 1:
                    i.then_inc(sem["dt_done"], 1)

            for h in range(2 * KT):
                transpose_x(0, h)
                if h == 2:
                    pe.wait_ge(sem["dtw_ready"], 1)
                if h >= 2:
                    rows_dt(0, h - 2)
            rows_dt(0, 2 * KT - 2)
            rows_dt(0, 2 * KT - 1)
            pe.wait_ge(sem["spread_ready"], 1)

            def spread_decay(b, k):
                if k >= 2:
                    pe.wait_ge(sem["scanned"], KT * b + k - 1)
                for n in range(2):
                    for low, decay in enumerate((decay_hi, decay_lo)):
                        i = nc.tensor.matmul(pair(C if b else A, k)[:, n, :], spread_s[:, k, :],
                                             decay[:, n * HALF:(n + 1) * HALF], start=not low, stop=low == 1)
                i.then_inc(sem["bc_done"], 1)

            def scan_back(b, k):
                pe.wait_ge(sem["scanned"], KT * b + k + 1)
                if k >= 2:
                    name, v = back_taken(b, k - 2)
                    pe.wait_ge(sem[name], v)
                dst = flat(pair(C, k))
                for st in range(ST):
                    i = nc.tensor.transpose(dst[:, st * P:(st + 1) * P], hs[:, k, st * P:(st + 1) * P], ident)
                i.then_inc(sem["back_done"], 1)

            pe.wait_ge(sem["decay_ready"], 4)
            for k in range(KT + 1):
                if k < KT:
                    spread_decay(0, k)
                if k:
                    scan_back(0, k - 1)
            for b in range(B):
                if b:
                    for k in range(BACKS + 2, KT):
                        scan_back(b, k)
                def transpose_fn(i):
                    n, k = i // KT, i % KT
                    if k == 0 and n == 0:
                        pe.wait_ge(sem["norm_act"], ACT_NORM * (b + 1))
                    elif k == 0:
                        pe.wait_ge(sem["norm_ready"], NORMS * (b + 1) - X_ACT)
                    if 4 <= i < KT:
                        pe.wait_ge(sem["fn_parts"], 2 * KT * b + i - 3)
                    elif i >= KT + 2:
                        pe.wait_ge(sem["fn_parts"], 2 * KT * b + i - 5)
                    for q in range(ST // 2):
                        ins = nc.tensor.transpose(fn_bank(i)[:, q * P:(q + 1) * P],
                                                  xn[:, n * ST // 2 + q, k * P:(k + 1) * P], ident)
                        if i == 0 and q == 0:
                            ins.then_inc(sem["tileC"], 1)
                    ins.then_inc(sem["fn_tr_done"], 1)

                pe.wait_ge(sem["radd_done"], back_taken(b, KT - 1)[1])
                for i in range(KT):
                    transpose_fn(i)

                def ff_round(g):
                    for i in (0, 2, 1, 3, 4, 5, 6, 7) if isinstance(g, int) else range(2 * JB):
                        j, n = i // 2, i % 2
                        if n == 0:
                            pe.wait_ge(sem["w_ready"], SLABS * b + slab_pos(g, j) + 1)
                        if not isinstance(g, int) or i >= 4:
                            pe.wait_ge(sem["gelu_parts"], TILES_FF * b + 8 * g + i - 3)
                        if isinstance(g, int) and i == 2:
                            transpose_fn(2 * KT - 2)
                            transpose_fn(2 * KT - 1)
                        if isinstance(g, int) and i == 1:
                            pe.wait_ge(sem["fn_parts"], 2 * KT * (b + 1) - 1)
                        slab_tile(i % 4, j % 2, n, before=feature_tile if isinstance(g, int) and i < 2 else None)
                    for st in range(ST):
                        v = ST * ROUNDS * b + ST * g + st
                        if not isinstance(v, int) or v >= 2:
                            pe.wait_ge(sem["yadded"], v - 1)
                        for j in range(JB):
                            if st == 0:
                                pe.wait_ge(sem["w_ready"], SLABS * b + 8 * g + W2_POS[j] + 1)
                                pe.wait_ge(sem["hid_split"], TILES_FF * b + 8 * g + 2 * j + 2)
                            s = slice(st * P, (st + 1) * P)
                            for n in range(2):
                                r = slice(n * HALF, (n + 1) * HALF)
                                ins = three(pair(C, st)[:, n, :], hid_hi[:, j, s], hid_lo[:, j, s], w2_hi[:, j, r],
                                            w2_lo[:, j, r], j == 0, j == JB - 1)
                        ins.then_inc(sem["tileC"], 1)

                def feature_tile(n, k):
                    pe.wait_ge(sem["fn_lo" if k % 2 else "fn_split"], KT * b + KT // 2 * n + k // 2 + 1)
                    if n == 0 and k >= 2:
                        transpose_fn(KT + k - 2)

                ff_round(0)
                with pe.Fori(1, ROUNDS) as g:
                    ff_round(g)

                def gp_tiles(o):
                    for w in range(2):
                        pe.wait_ge(sem["w_ready"], SLABS * b + 2 * W1_SLABS + 2 * o + w + 1)
                        if isinstance(o, int):
                            pe.wait_ge(sem["gelu_parts"], TILES_FF * (b + 1))
                        elif w == 0:
                            pe.wait_ge(sem["g_ready"], 2 * OT * b + 2 * o)
                        else:
                            pe.wait_ge(sem["p_used"], OT * b + o)
                        for n in range(2):
                            for k in range(KT):
                                if isinstance(o, int) and w == 0 and n == 0:
                                    pe.wait_ge(sem["x1_split"], ST * b + k + 1)
                                c = slice(k * P, (k + 1) * P)
                                r = slice(n * HALF, (n + 1) * HALF)
                                ins = three(A[:, 2 * w + n, :], w1_hi[:, w, c], w1_lo[:, w, c], act_hi[b][:, k, r],
                                            act_lo[:, k, r], k == 0, k == KT - 1)
                            ins.then_inc(sem["tileA"], 1)

                gp_tiles(0)
                with pe.Fori(1, OT) as o:
                    gp_tiles(o)

                def t_tile(o, i):
                    if i % 2 == 0:
                        pe.wait_ge(sem["w_ready"], SLABS * b + 2 * W1_SLABS + 2 * OT + o + 1)
                    slab_tile(i % 4, (i // 2) % 2, i % 2)

                pe.wait_ge(sem["g_ready"], 2 * OT * (b + 1))
                for i in range(2):
                    t_tile(0, i)
                pe.wait_ge(sem["s3_ready"], b + 1)
                nc.tensor.matmul(C[:, 0, 0:3], ones[:], s3[:, 0:3], start=True, stop=True).then_inc(sem["tot_done"], 1)
                pe.wait_ge(sem["p_used"], OT * (b + 1))
                for i in range(2, 2 * OT):
                    if i >= 4:
                        pe.wait_ge(sem["t_used"], 2 * OT * b + i - 3)
                    t_tile(i // 2, i)
                for i in range(2 * ST):
                    q, sub, n = i // 4, (i // 2) % 2, i % 2
                    if i % 4 == 0:
                        pe.wait_ge(sem["w_ready"], SLABS * b + 2 * W1_SLABS + 3 * OT + q + 1)
                    if i < 4:
                        pe.wait_ge(sem["t_used"], 2 * OT * (b + 1) - 3 + i)
                    else:
                        pe.wait_ge(sem["z_ready"], 2 * ST * b + i - 3)
                    for k in range(OT):
                        if i < 2:
                            pe.wait_ge(sem["y_split"], 2 * OT * b + 2 * k + n + 1)
                        c = slice(k * 2 * P + sub * P, k * 2 * P + (sub + 1) * P)
                        r = slice(n * HALF, (n + 1) * HALF)
                        ins = three(A[:, i % 4, :], w1_hi[:, q % 2, c], w1_lo[:, q % 2, c], hid_hi[:, k, r],
                                    hid_lo[:, k, r], k == 0, k == OT - 1)
                    ins.then_inc(sem["tileA"], 1)
                    if b + 1 < B and TR_AT <= i < TR_AT + KT:
                        for h in (2 * (i - TR_AT), 2 * (i - TR_AT) + 1):
                            transpose_x(b + 1, h)
                            if h >= 2:
                                rows_dt(b + 1, h - 2)
                    if b + 1 < B and i == TR_AT + KT - 1:
                        rows_dt(b + 1, 2 * KT - 2)
                        rows_dt(b + 1, 2 * KT - 1)
                    if b + 1 < B and i >= BACK_AT:
                        if i == BACK_AT:
                            pe.wait_ge(sem["scanned"], KT * (b + 2))
                        scan_back(b + 1, 2 * (i - BACK_AT))
                        scan_back(b + 1, 2 * (i - BACK_AT) + 1)
                    elif b + 1 < B and i >= BC_AT:
                        if i == BC_AT:
                            pe.wait_ge(sem["decay_ready"], 4 * (b + 2))
                        spread_decay(b + 1, 2 * (i - BC_AT))
                        spread_decay(b + 1, 2 * (i - BC_AT) + 1)
                if b + 1 < B:
                    scan_back(b + 1, BACKS)
                    scan_back(b + 1, BACKS + 1)
                pe.wait_ge(sem["zmv_ready"], b + 1)
                nc.tensor.matmul(A[:, 3, 0:2], ones[:], zmv[:, 0:2], start=True, stop=True).then_inc(sem["mu_done"], 1)
                pe.wait_ge(sem["zw_ready"], b + 1)
                nc.tensor.matmul(A[:, 3, 8:9], ones[:], zw[:, 0:1], start=True, stop=True).then_inc(sem["var_done"], 1)


def kernel(**inputs):
    import numpy as np
    import concourse.bacc as bacc
    from concourse.bass_utils import run_bass_kernel_spmd

    v = {k: np.asarray(a) for k, a in inputs.items()}

    def slab(wt, width):
        r, c = wt.shape
        return wt.reshape(r // P, P, c // width, width).transpose(2, 1, 0, 3).reshape(c // width, P, r // P * width)

    wt, wp, wg, wz = (v["L1_conv_" + n].T for n in ("Wt", "Wp", "Wg", "Wz"))
    gp = np.stack([slab(wg, P), slab(wp, P)], axis=1).reshape(2 * OT, P, ED)
    by_tile = lambda a: a.reshape(-1, P).T
    eye = np.eye(P, dtype=np.float32)
    row_of = (np.arange(ED) // D)
    onehot = (row_of[:, None] == np.arange(D)[None, :]).astype(np.float32)
    arrays = {
        "x": v["x"].reshape(B, S, ED),
        "slabs": np.concatenate([slab(v["L0_conv_W1"], P), gp, slab(wt, P), slab(wz, 2 * P)], axis=0),
        "w2": v["L0_conv_W2"].reshape(W1_SLABS, P, ED),
        "cols": np.concatenate([by_tile(v[n].reshape(-1)) for n in (
            "L0_conv_g_ssm", "L0_conv_b_ssm", "L0_conv_g_ffn", "L0_conv_b_ffn", "L0_conv_bb1",
            "L1_conv_gn_w", "L1_conv_gn_b")], axis=1),
        "bb2": v["L0_conv_bb2"].reshape(ED),
        "w_dt": v["L0_conv_w_dt"].reshape(D, 1),
        "log_a": v["L0_conv_log_A"].reshape(D, 1),
        "b_dt": v["L0_conv_b_dt"].reshape(1),
        "consts": np.concatenate([eye, onehot.reshape(KT, P, D).transpose(1, 0, 2).reshape(P, KT * D)], axis=1),
        "spread": np.concatenate([onehot.T] * RPT, axis=0),
    }
    arrays = {k: np.ascontiguousarray(a) for k, a in arrays.items()}
    nc = bacc.Bacc("TRN2", target_bir_lowering=False, num_devices=1)
    args = [nc.dram_tensor(k, a.shape, mybir.dt.from_np(a.dtype), kind="ExternalInput").ap() for k, a in arrays.items()]
    out = nc.dram_tensor("out", (B, S, ED), F32, kind="ExternalOutput").ap()
    build(nc, *args, out)
    r = run_bass_kernel_spmd(nc, [arrays], core_ids=[0])
    return r.results[0]["out"].reshape(B, S, D, D)
```
